# Optimizing a Trainium2 kernel written in Bass

```python
import numpy as np
import jax
import jax.numpy as jnp

def _softmax(x, axis=-1):
    return jax.nn.softmax(x, axis=axis)

def _gelu(x):
    return jax.nn.gelu(x, approximate=True)

def _silu(x):
    return jax.nn.silu(x)

def _sigmoid(x):
    return jax.nn.sigmoid(x)

def _layernorm(x, axis=-1, eps=1e-05):
    m = jnp.mean(x, axis=axis, keepdims=True)
    v = jnp.var(x, axis=axis, keepdims=True)
    return (x - m) / jnp.sqrt(v + eps)

def _scatter_add(tgt, idx, src, axis=0):
    return tgt.at[idx].add(src)

def _segment_sum(src, seg, n):
    return jax.ops.segment_sum(src, seg, n)
kernel_name = 'mk_recurrent_d1_jaxref_r8_dd72ae'

def setup_inputs(seed: int=0):
    np.random.seed(seed)
    _w = jnp.asarray

    def _L0_attn_setup():
        import jax, jax.numpy as jnp
        import numpy as np
        DIM = 512
        N_HEADS = 32
        HEAD_DIM = DIM // N_HEADS
        key = jax.random.key(seed)
        k0, k1, k2, k3, k4 = jax.random.split(key, 5)
        B, T = (2, 256)
        x = jax.random.normal(k0, (B, T, DIM), dtype=jnp.float32)
        s = 1.0 / np.sqrt(DIM)
        wq = jax.random.normal(k1, (DIM, DIM), dtype=jnp.float32) * s
        wk = jax.random.normal(k2, (DIM, HEAD_DIM), dtype=jnp.float32) * s
        wv = jax.random.normal(k3, (DIM, HEAD_DIM), dtype=jnp.float32) * s
        wo = jax.random.normal(k4, (DIM, DIM), dtype=jnp.float32) * s
        return {'x': x, 'wq': wq, 'wk': wk, 'wv': wv, 'wo': wo}
    _L0_attn_in = _L0_attn_setup()

    def _L0_ffn_setup():
        import jax, jax.numpy as jnp
        import numpy as np
        DIM = 512
        HID = 1376
        R = 16
        SCALING = 32.0 / 16.0

        def _lora_linear(x, w, a, b):
            base = jnp.einsum('bsd,od->bso', x, w)
            low = jnp.einsum('bsr,or->bso', jnp.einsum('bsd,rd->bsr', x, a), b)
            return base + low * SCALING
        key = jax.random.key(seed)
        ks = jax.random.split(key, 10)
        s_in = 1.0 / np.sqrt(DIM)
        s_hid = 1.0 / np.sqrt(HID)
        return {'x': jax.random.normal(ks[0], (4, 256, DIM), jnp.float32), 'w1': jax.random.normal(ks[1], (HID, DIM), jnp.float32) * s_in, 'w3': jax.random.normal(ks[2], (HID, DIM), jnp.float32) * s_in, 'w2': jax.random.normal(ks[3], (DIM, HID), jnp.float32) * s_hid, 'lora_A1': jax.random.normal(ks[4], (R, DIM), jnp.float32) * s_in, 'lora_B1': jax.random.normal(ks[5], (HID, R), jnp.float32) * 0.02, 'lora_A3': jax.random.normal(ks[6], (R, DIM), jnp.float32) * s_in, 'lora_B3': jax.random.normal(ks[7], (HID, R), jnp.float32) * 0.02, 'lora_A2': jax.random.normal(ks[8], (R, HID), jnp.float32) * s_hid, 'lora_B2': jax.random.normal(ks[9], (DIM, R), jnp.float32) * 0.02}
    _L0_ffn_in = _L0_ffn_setup()
    _d = {'L0_attn_x': _L0_attn_in['x'], 'L0_attn_wq': _L0_attn_in['wq'], 'L0_attn_wk': _L0_attn_in['wk'], 'L0_attn_wv': _L0_attn_in['wv'], 'L0_attn_wo': _L0_attn_in['wo'], 'L0_ffn_w1': _L0_ffn_in['w1'], 'L0_ffn_w3': _L0_ffn_in['w3'], 'L0_ffn_w2': _L0_ffn_in['w2'], 'L0_ffn_lora_A1': _L0_ffn_in['lora_A1'], 'L0_ffn_lora_B1': _L0_ffn_in['lora_B1'], 'L0_ffn_lora_A3': _L0_ffn_in['lora_A3'], 'L0_ffn_lora_B3': _L0_ffn_in['lora_B3'], 'L0_ffn_lora_A2': _L0_ffn_in['lora_A2'], 'L0_ffn_lora_B2': _L0_ffn_in['lora_B2']}
    _x0 = _d['L0_attn_x']
    _d['L0_attn_x'] = jax.random.normal(jax.random.fold_in(jax.random.key(seed), 1), (4, 256, 512), dtype=_x0.dtype)
    del _x0
    return _d

def reference(L0_attn_x, L0_attn_wq, L0_attn_wk, L0_attn_wv, L0_attn_wo, L0_ffn_w1, L0_ffn_w3, L0_ffn_w2, L0_ffn_lora_A1, L0_ffn_lora_B1, L0_ffn_lora_A3, L0_ffn_lora_B3, L0_ffn_lora_A2, L0_ffn_lora_B2):

    def _L0_attn_ref(x, wq, wk, wv, wo):
        import jax, jax.numpy as jnp
        import numpy as np
        DIM = 512
        N_HEADS = 32
        HEAD_DIM = DIM // N_HEADS
        B, T, C = x.shape
        q = (x @ wq).reshape(B, T, N_HEADS, HEAD_DIM)
        k = x @ wk
        v = x @ wv
        scale = 1.0 / jnp.sqrt(jnp.asarray(HEAD_DIM, dtype=x.dtype))
        scores = jnp.einsum('bqhd,bkd->bhqk', q, k) * scale
        causal = jnp.tril(jnp.ones((T, T), dtype=bool))
        scores = jnp.where(causal[None, None], scores, -jnp.inf)
        probs = jax.nn.softmax(scores.astype(jnp.float32), axis=-1).astype(x.dtype)
        out = jnp.einsum('bhqk,bkd->bqhd', probs, v).reshape(B, T, C)
        return out @ wo

    def _L0_ffn_ref(x, w1, w3, w2, lora_A1, lora_B1, lora_A3, lora_B3, lora_A2, lora_B2):
        import jax, jax.numpy as jnp
        import numpy as np
        DIM = 512
        HID = 1376
        R = 16
        SCALING = 32.0 / 16.0

        def _lora_linear(x, w, a, b):
            base = jnp.einsum('bsd,od->bso', x, w)
            low = jnp.einsum('bsr,or->bso', jnp.einsum('bsd,rd->bsr', x, a), b)
            return base + low * SCALING
        h1 = _lora_linear(x, w1, lora_A1, lora_B1)
        h3 = _lora_linear(x, w3, lora_A3, lora_B3)
        g = jax.nn.silu(h1) * h3
        return _lora_linear(g, w2, lora_A2, lora_B2)
    x = L0_attn_x
    xn = _layernorm(x, axis=-1)
    s = _L0_attn_ref(xn, L0_attn_wq, L0_attn_wk, L0_attn_wv, L0_attn_wo)
    g = _silu(_L0_ffn_ref(xn, L0_ffn_w1, L0_ffn_w3, L0_ffn_w2, L0_ffn_lora_A1, L0_ffn_lora_B1, L0_ffn_lora_A3, L0_ffn_lora_B3, L0_ffn_lora_A2, L0_ffn_lora_B2))
    x = x + s * g
    return x

_drawn_inputs = setup_inputs


def setup_inputs(seed=0):
    import zlib

    import numpy as np

    out = dict(_drawn_inputs(seed))
    spreads = {}
    factors = {'L0_ffn_lora_A1': 4.384,
     'L0_ffn_lora_B1': 4.384,
     'L0_ffn_lora_A3': 3.008,
     'L0_ffn_lora_B3': 3.193,
     'L0_ffn_lora_A2': 3.146,
     'L0_ffn_lora_B2': 3.193}
    for name, (base, spread) in spreads.items():
        noise = np.random.default_rng([zlib.crc32(name.encode()), seed]).standard_normal(out[name].shape)
        drawn = base * np.exp(spread * noise) if base else spread * noise
        out[name] = jnp.asarray(drawn.astype(out[name].dtype))
    for name, factor in factors.items():
        out[name] = (out[name] * factor).astype(out[name].dtype)
    return out
```

```python
from contextlib import ExitStack

import numpy as np

import concourse.bass as bass
from concourse import mybir

F32 = mybir.dt.float32
F32R = mybir.dt.float32r
BF16 = mybir.dt.bfloat16
ALU = mybir.AluOpType
ACT = mybir.ActivationFunctionType
AX = mybir.AxisListType

P = 128
BATCH, SEQ, DIM = 4, 256, 512
TOK = BATCH * SEQ
HALF = TOK // 2
HID, RANK = 1376, 16
HEADS, HDIM = 32, 16
DT = DIM // P
HT = -(-HID // P)
HLAST = HID - (HT - 1) * P
LORA_SCALE = 2.0
LN_EPS = 1e-5
SCORE_SCALE = float(HDIM) ** -0.5
NEG = -1.0e30
UNITS = BATCH * HEADS // 8
RAW_RING = 4
AUX0, AUX_RING = 4, 4
KV_ROWS = 6 * HDIM + HDIM
Q_DMAS = 12
KROWS = 100


def hid_rows(t):
    return P if t < HT - 1 else HLAST


def unit(u):
    return u // 8, (u % 8) // 2, u % 2


def plan():
    steps = [("ln", 0), ("w", "wkv", 0), ("w", "wq", 0)]
    steps += [("xt", i) for i in range(4)]
    steps += [("ln", 1), ("kv", 0)]
    steps += [("xt", i) for i in range(4, 8)]
    steps += [("ba", "w1", 0), ("ba", "w3", 0), ("q", 0), ("kv", 1), ("vt", 0), ("vt", 1)]
    atoms = [("ffn1", t, i) for t in range(HT) for i in range(16)]
    per_slot = 10
    at = 0
    for s in range(UNITS + 2):
        for k in range(per_slot):
            if at < len(atoms):
                _, t, i = atoms[at]
                steps.append(atoms[at])
                at += 1
                if t + 1 < HT and i == 3:
                    steps.append(("ba", "w1", t + 1))
                if t + 1 < HT and i == 7:
                    steps.append(("ba", "w3", t + 1))
            a, b, c = s, s - 1, s - 2
            if 0 <= c < UNITS:
                steps += {0: [("pv", c)], 3: [("olt", c)], 5: [("ot", c)]}.get(k, [])
            if a < UNITS:
                steps += {0: [("max", a, 0)], 1: [("max", a, 1)], 3: [("max", a, 2)],
                          4: [("max", a, 3)], 6: [("max", a, 4)], 7: [("max", a, 5)],
                          9: [("mrow", a, 0), ("mrow", a, 1)]}.get(k, [])
            if 0 <= b < UNITS:
                steps += {2: [("exp", b, 0)], 4: [("exp", b, 1)], 5: [("exp", b, 2)],
                          6: [("exp", b, 3)], 7: [("exp", b, 4)], 8: [("exp", b, 5)]}.get(k, [])
            if s % 2 == 0 and s // 2 + 1 < UNITS // 2:
                if k == 2 and s // 2 + 1 < 4:
                    steps.append(("w", "wq", s // 2 + 1))
                if k == 8:
                    steps.append(("q", s // 2 + 1))
            if s >= UNITS - 2 and k == 6:
                steps.append(("ba", "w2", s - UNITS + 2))
    for half in range(2):
        for k in range(HT):
            if half == 0 and k + 4 < HT:
                steps.append(("ba", "w2", k + 4))
            if half == 0 and k == 0:
                steps += [("gsplit", 0, 0), ("gsplit", 0, 1)]
            n = half * HT + k + 2
            if n < 2 * HT:
                steps.append(("gsplit", n // HT, n % HT))
            if half == 0 and k >= HT - 4:
                steps += [("w", "wo", k - HT + 4), ("osplit", 0, k - HT + 4)]
            if half == 1 and 1 <= k < 5:
                steps.append(("osplit", 1, k - 1))
            if half == 1 and 5 <= k < 9:
                steps.append(("wo", 1, k - 5))
            steps += [("ffn2", half, k, d) for d in range(DT)]
        if half == 0:
            steps += [("wo", 0, d) for d in range(DT)]
        steps += [("fin", half, d) for d in range(DT)]
    return steps


AUX_JOBS = {"xt", "kv", "vt", "ba", "q", "max", "mrow", "exp", "pv", "olt", "ot", "wo"}


def number(steps, kinds):
    return {s: n for n, s in enumerate(s for s in steps if s[0] in kinds)}


def mixed_block_kernel(nc, x, xT, wq, wkv, wo, w1, w1_last, w3, w3_last, w2T,
                       lora_a, lora_b, consts, outT):
    steps = plan()
    aux_no = number(steps, AUX_JOBS)
    aux_steps = list(aux_no)
    split_no = number(steps, {"w", "ba"})
    merged_no = number(steps, {"ba"})
    raw_steps = [s for s in steps if s[0] in ("w", "ba", "fin")]
    raw_no = {s: n for n, s in enumerate(raw_steps)}

    with ExitStack() as ctx:
        def sb(name, shape, dt=F32):
            return ctx.enter_context(nc.sbuf_tensor(name, shape, dt))

        def sem(name):
            return ctx.enter_context(nc.semaphore(name))

        bank = [ctx.enter_context(nc.psum_tensor(f"bank{i}", [P, 512], F32)) for i in range(8)]

        ident = sb("ident", [P, P])
        ident_b = sb("ident_b", [P, P], BF16)
        mask_f = sb("mask_f", [P, P])
        mask_b = sb("mask_b", [P, 4, P], BF16)
        sel = sb("sel", [P, 2])
        lora1 = sb("lora1", [P, HID])
        lora2 = sb("lora2", [P, DIM])
        raw = sb("raw", [P, RAW_RING, 512])
        weff = sb("weff", [P, 2, 512])
        xsplit = sb("xsplit", [P, 2, DT, TOK], F32R)
        wq_s = sb("wq_s", [P, 4, 2, 512], F32R)
        wkv_s = sb("wkv_s", [P, 2, DT, KV_ROWS], F32R)
        w13 = sb("w13", [P, 2, 2, 2, 512], F32R)
        g = sb("g", [P, HT, TOK])
        u_t = sb("u_t", [P, 2, 512])
        g1 = sb("g1", [P, 512])
        qsplit = sb("qsplit", [P, 2, 2, 512], F32R)
        stack = [sb(f"stack{i}", [P, 4, 512], F32R) for i in range(2)]
        kst = sb("kst", [P, 2, TOK], F32R)
        vext = sb("vext", [P, 8, 32])
        negmax = sb("negmax", [P, 2, 4, 2])
        msplit = sb("msplit", [P, 2, 4, 4], F32R)
        p0 = sb("p0", [P, 2, 2, 2, SEQ])
        p1 = sb("p1", [P, 2, 4, P])
        ol = sb("ol", [P, 512])
        rden = sb("rden", [P, 2, 2, 4])
        on = sb("on", [P, 2, P])
        oT = sb("oT", [P, 4, TOK])
        stats = sb("stats", [P, 8, 6])
        mv = sb("mv", [P, 8, 2])
        lnv = sb("lnv", [P, 5, 8])
        y = p0[:].rearrange("p a e b q -> p (a e b q)").rearrange("p (n t) -> p n t", n=4)

        const_in = sem("const_in")
        lora_in = sem("lora_in")
        x_in = [sem(f"x_in{h}") for h in range(2)]
        raw_in = [sem(f"raw_in{i}") for i in range(RAW_RING)]
        q_moved = [sem(f"q_moved{i}") for i in range(2)]
        y_out = [sem(f"y_out{i}") for i in range(4)]
        aux_filled = sem("aux_filled")
        consts_ready = sem("consts_ready")
        var_ready = sem("var_ready")
        std_ready = sem("std_ready")
        xn_ready = sem("xn_ready")
        xhi_ready = sem("xhi_ready")
        xlo_ready = sem("xlo_ready")
        kv_copied = sem("kv_copied")
        k_ready = sem("k_ready")
        v_ready = sem("v_ready")
        merged = sem("merged")
        max_done = sem("max_done")
        s_read = sem("s_read")
        w_hi = sem("w_hi")
        w_lo = sem("w_lo")
        h_ready = sem("h_ready")
        tanh_done = sem("tanh_done")
        gate_done = sem("gate_done")
        q_hi = sem("q_hi")
        q_lo = sem("q_lo")
        m_ready = sem("m_ready")
        mrow_ready = sem("mrow_ready")
        exp_done = sem("exp_done")
        p_masked = sem("p_masked")
        ol_ready = sem("ol_ready")
        on_ready = sem("on_ready")
        oT_ready = sem("oT_ready")
        g_hi = sem("g_hi")
        g_lo = sem("g_lo")
        o_hi = sem("o_hi")
        o_lo = sem("o_lo")
        f_step = sem("f_step")
        f_ready = sem("f_ready")
        ftanh = sem("ftanh")
        f_read = sem("f_read")
        y_ready = sem("y_ready")
        chain = sem("chain")

        def x_tile(i):
            return g[:, 7 + i // 2, (i % 2) * 512:(i % 2) * 512 + 512]

        def xn_tile(i):
            return g[:, 3 + i // 2, (i % 2) * 512:(i % 2) * 512 + 512]

        kv_rows = g[0:KV_ROWS, 2, :]

        def wait_read(eng, step):
            kind, *at = step
            last_reader = {
                "xt": lambda i: (xlo_ready, i + 1),
                "kv": lambda half: (k_ready, half + 1),
                "vt": lambda half: (v_ready, half + 1),
                "ba": lambda name, i: (merged, merged_no[step] + 1),
                "q": lambda k: (q_lo, k + 1),
                "max": lambda u, k: (max_done, 6 * u + k + 1),
                "mrow": lambda u, qt: (mrow_ready, 2 * u + qt + 1),
                "exp": lambda u, k: (exp_done, 6 * u + k + 1),
                "pv": lambda u: (ol_ready, u + 1),
                "olt": lambda u: (on_ready, u + 1),
                "ot": lambda u: (oT_ready, u + 1),
                "wo": lambda half, d: (s_read, DT * half + d + 1),
            }
            eng.wait_ge(*last_reader[kind](*at))

        def wait_filled(eng, step):
            eng.wait_ge(aux_filled, aux_no[step] + 1)

        def aux(step):
            return bank[AUX0 + aux_no[step] % AUX_RING]

        def split_dst(step, part):
            _, name, i = step
            if name == "wkv":
                return wkv_s[:, part]
            if name == "wq":
                return wq_s[:, i, part, :]
            if name == "wo":
                return stack[part][:, i, :]
            if name == "w2":
                if i < 4:
                    return wq_s[0:hid_rows(i), i, part, :]
                j = i - 4
                return xsplit[0:hid_rows(i), part, j // 2, (j % 2) * 512:(j % 2) * 512 + 512]
            m = hid_rows(i)
            tile = w13[:, i % 2, 0 if name == "w1" else 1, part, :]
            return tile.rearrange("p (c m) -> p c m", c=DT)[:, :, 0:m]

        def split_src(step):
            kind, name, i = step
            if kind == "ba":
                tile = weff[:, merged_no[step] % 2, :]
            else:
                tile = raw[:, raw_no[step] % RAW_RING, :]
            if name == "wkv":
                return tile[:, 0:DT * KV_ROWS].rearrange("p (c m) -> p c m", c=DT)
            if name in ("wq", "wo"):
                return tile
            return cut(tile, name, i)

        def cut(tile, name, i):
            if name == "w2":
                return tile[0:hid_rows(i)]
            return tile.rearrange("p (c m) -> p c m", c=DT)[:, :, 0:hid_rows(i)]

        def g_entry(half, k, part):
            n = (half * HT + k) % 4
            return w13[0:hid_rows(k), (n // 2 + 1) % 2, n % 2, part, :]

        def g_src(half, k):
            return g[0:hid_rows(k), k, half * HALF:(half + 1) * HALF]

        def o_hi_tile(o):
            return kst[:, o // 2, (o % 2) * 512:(o % 2) * 512 + 512]

        def o_lo_tile(o):
            return qsplit[:, o // 2, o % 2, :]

        block = ctx.enter_context(nc.Block())

        @block.sync
        def _(sp):
            for i in range(4):
                sp.dma_start(x_tile(i), x[i * P:(i + 1) * P, :]).then_inc(x_in[0], 16)
            sp.dma_start(ident[:], consts[:, 0:P]).then_inc(const_in, 16)
            sp.dma_start(mask_f[:], consts[:, P:2 * P]).then_inc(const_in, 16)
            sp.dma_start(sel[:], consts[:, 2 * P:2 * P + 2]).then_inc(const_in, 16)

            def load_raw(step):
                n = raw_no[step]
                if n >= RAW_RING:
                    old = raw_steps[n - RAW_RING]
                    if old[0] == "w":
                        sp.wait_ge(w_lo, split_no[old] + 1)
                    elif old[0] == "ba":
                        sp.wait_ge(merged, merged_no[old] + 1)
                    else:
                        sp.wait_ge(y_ready, old[1] * DT + old[2] + 1)
                kind, name, i = step
                tile = raw[:, n % RAW_RING, :]
                if kind == "fin":
                    half, d = name, i
                    src = xT[d * P:(d + 1) * P, half * HALF:(half + 1) * HALF]
                    dst = tile
                elif name == "wkv":
                    src, dst = wkv, tile[:, 0:DT * KV_ROWS]
                elif name == "wq":
                    src, dst = wq[i], tile
                elif name == "wo":
                    src, dst = wo[i * P:(i + 1) * P, :], tile
                elif name == "w2":
                    src, dst = w2T[i * P:i * P + hid_rows(i), :], tile[0:hid_rows(i)]
                else:
                    main, last = (w1, w1_last) if name == "w1" else (w3, w3_last)
                    if i < HT - 1:
                        src, dst = main[i], tile
                    else:
                        src, dst = last, cut(tile, name, i)
                sp.dma_start(dst, src).then_inc(raw_in[n % RAW_RING], 16)

            def move_queries(k):
                sp.wait_ge(q_lo, k + 1)
                if k >= 2:
                    wait_filled(sp, ("exp", 2 * (k - 2) + 1, 5))
                for blk, part in enumerate((0, 1, 0)):
                    for j in range(4):
                        sp.dma_start(stack[k % 2][32 * blk:32 * blk + 32, j, :].bitcast(F32),
                                     qsplit[32 * j:32 * j + 32, k % 2, part, :].bitcast(F32)
                                     ).then_inc(q_moved[k % 2], 16)

            for n in range(2):
                load_raw(raw_steps[n])
            for i in range(4, 8):
                sp.dma_start(x_tile(i), x[i * P:(i + 1) * P, :]).then_inc(x_in[1], 16)
            for r in range(3):
                sp.dma_start(lora1[32 * r:32 * r + RANK, :], lora_b[r]).then_inc(lora_in, 16)
                sp.dma_start(lora2[32 * r:32 * r + RANK, :], lora_a[r]).then_inc(lora_in, 16)
            for n in range(2, RAW_RING):
                load_raw(raw_steps[n])
            for step in steps:
                if step in raw_no and raw_no[step] + RAW_RING < len(raw_steps):
                    load_raw(raw_steps[raw_no[step] + RAW_RING])
                if step[0] == "q":
                    move_queries(step[1])
                if step[0] == "fin":
                    _, half, d = step
                    sp.wait_ge(y_ready, half * DT + d + 1)
                    sp.dma_start(outT[d * P:(d + 1) * P, half * HALF:(half + 1) * HALF],
                                 y[:, d, :]).then_inc(y_out[d], 16)
            for d in range(DT):
                sp.wait_ge(y_out[d], 32)

        @block.tensor
        def _(pe):
            def take_bank(step):
                n = aux_no[step]
                if n >= AUX_RING:
                    wait_read(pe, aux_steps[n - AUX_RING])
                return aux(step)

            def three_passes(out, w_parts, m_parts, start, stop):
                pe.matmul(out, w_parts[0], m_parts[0], start=start, stop=False)
                pe.matmul(out, w_parts[0], m_parts[1], start=False, stop=False)
                return pe.matmul(out, w_parts[1], m_parts[0], start=False, stop=stop)

            def x_parts(c, half):
                return [xsplit[:, part, c, half * HALF:(half + 1) * HALF] for part in (0, 1)]

            def xt(step):
                i = step[1]
                ps = take_bank(step)
                pe.wait_ge(xn_ready, i + 1)
                for c in range(DT):
                    mm = pe.transpose(ps[:, c * P:(c + 1) * P], xn_tile(i)[:, c * P:(c + 1) * P], ident[:])
                mm.then_inc(aux_filled, 1)

            def kv(step):
                half = step[1]
                ps = take_bank(step)
                pe.wait_ge(w_lo, split_no[("w", "wkv", 0)] + 1)
                pe.wait_ge(xlo_ready, 4 * (half + 1))
                for c in range(DT):
                    mm = three_passes(ps[0:KV_ROWS, :], [wkv_s[:, part, c, :] for part in (0, 1)],
                                      x_parts(c, half), c == 0, c == DT - 1)
                mm.then_inc(aux_filled, 1)

            def vt(step):
                half = step[1]
                ps = take_bank(step)
                pe.wait_ge(kv_copied, half + 1)
                for i in range(4):
                    t0 = half * HALF + i * P
                    mm = pe.transpose(ps[:, i * KV_ROWS:(i + 1) * KV_ROWS], kv_rows[:, t0:t0 + P],
                                      ident[0:KV_ROWS, 0:KV_ROWS])
                mm.then_inc(aux_filled, 1)

            def ba(step):
                _, name, i = step
                ps = take_bank(step)
                m = hid_rows(i)
                if name == "w2":
                    mm = pe.matmul(ps[0:m, :], lora1[64:64 + RANK, i * P:i * P + m],
                                   lora2[64:64 + RANK, :], start=True, stop=True)
                else:
                    r = 0 if name == "w1" else 32
                    for c in range(DT):
                        mm = pe.matmul(ps[:, c * P:c * P + m], lora2[r:r + RANK, c * P:(c + 1) * P],
                                       lora1[r:r + RANK, i * P:i * P + m], start=True, stop=True)
                mm.then_inc(aux_filled, 1)

            def q(step):
                half, o, _ = unit(2 * step[1])
                ps = take_bank(step)
                pe.wait_ge(w_lo, split_no[("w", "wq", o)] + 1)
                for c in range(DT):
                    mm = three_passes(ps[:, :], [wq_s[:, o, part, c * P:(c + 1) * P] for part in (0, 1)],
                                      x_parts(c, half), c == 0, c == DT - 1)
                mm.then_inc(aux_filled, 1)

            def ffn1(step):
                _, t, i = step
                half, w, c = i // 8, (i // 4) % 2, i % 4
                m = hid_rows(t)
                if i == 0:
                    pe.wait_ge(w_lo, split_no[("ba", "w1", t)] + 1)
                if i == 4:
                    pe.wait_ge(w_lo, split_no[("ba", "w3", t)] + 1)
                if t == 0 and i % 8 == 0:
                    pe.wait_ge(xlo_ready, 4 * (half + 1))
                if c == 0 and t >= 1:
                    pe.wait_ge(gate_done, 2 * (t - 1) + half + 1)
                ps = bank[2 * half + w]
                mm = three_passes(ps[0:m, :], [w13[:, t % 2, w, part, c * P:c * P + m] for part in (0, 1)],
                                  x_parts(c, half), c == 0, c == DT - 1)
                if c == DT - 1:
                    mm.then_inc(h_ready, 1)

            def causal_scores(step):
                _, u, k = step
                half, o, b2 = unit(u)
                kcol = (2 * half + b2) * SEQ
                st = stack[(u // 2) % 2]
                ps = take_bank(step)
                if k == 0:
                    pe.wait_ge(q_moved[(u // 2) % 2], 16 * Q_DMAS * (u // 4 + 1))
                    if u == 0:
                        pe.wait_ge(k_ready, 2)
                        pe.wait_ge(consts_ready, 1)
                if k < 4:
                    pe.matmul(ps[:, :], st[0:96, k, b2 * SEQ + P:b2 * SEQ + 2 * P],
                              kst[0:96, :, kcol:kcol + SEQ], start=True, stop=False)
                    mm = pe.matmul(ps[:].rearrange("p (e k) -> p e k", e=2)[:, :, P:2 * P], ident_b[:],
                                   mask_b[:, 0:2, :], start=False, stop=True)
                else:
                    for n in range(2):
                        pe.matmul(ps[:, 256 * n:256 * n + 256],
                                  st[0:96, 2 * (k - 4) + n, b2 * SEQ:b2 * SEQ + P],
                                  kst[0:96, :, kcol:kcol + P], start=(n == 0), stop=False,
                                  skip_group_check=True)
                    mm = pe.matmul(ps[:, :], ident_b[:], mask_b[:], start=False, stop=True,
                                   skip_group_check=True)
                mm.then_inc(aux_filled, 1)

            def max_rows(step):
                _, u, qt = step
                ps = take_bank(step)
                pe.wait_ge(m_ready, u + 1)
                for j in range(4):
                    mm = pe.transpose(ps[0:4, j * P:(j + 1) * P], msplit[:, qt, j, :].bitcast(F32), ident[:])
                mm.then_inc(aux_filled, 1)

            def shifted_scores(step):
                _, u, k = step
                half, o, b2 = unit(u)
                kcol = (2 * half + b2) * SEQ
                st = stack[(u // 2) % 2]
                ps = take_bank(step)
                if k == 0:
                    pe.wait_ge(mrow_ready, 2 * (u + 1))
                if k < 2:
                    mm = pe.matmul(ps[:, :], kst[0:KROWS, k, kcol + P:kcol + 2 * P],
                                   st[0:KROWS, :, b2 * SEQ + P:b2 * SEQ + 2 * P], start=True, stop=True)
                else:
                    pp, e = (k - 2) // 2, (k - 2) % 2
                    mm = pe.matmul(ps[:, :], kst[0:KROWS, e, kcol:kcol + P],
                                   st[0:KROWS, 2 * pp:2 * pp + 2, b2 * SEQ:(b2 + 1) * SEQ],
                                   start=True, stop=True)
                mm.then_inc(aux_filled, 1)

            def pv(step):
                u = step[1]
                half, o, b2 = unit(u)
                kt = 2 * (2 * half + b2)
                ps = take_bank(step)
                if u == 0:
                    pe.wait_ge(v_ready, 2)
                pe.wait_ge(p_masked, 3 * (u + 1))
                for j in range(4):
                    pe.matmul(ps[32 * j:32 * j + 32, :], vext[:, kt, :], p0[:, j // 2, :, j % 2, :],
                              start=True, stop=False)
                for j in range(4):
                    out = ps[32 * j:32 * j + 32, :].rearrange("p (e q) -> p e q", e=2)[:, :, P:2 * P]
                    mm = pe.matmul(out, vext[:, kt + 1, :], p1[:, :, j, :], start=False, stop=True)
                mm.then_inc(aux_filled, 1)

            def olt(step):
                u = step[1]
                ps = take_bank(step)
                pe.wait_ge(ol_ready, u + 1)
                for n in range(4):
                    mm = pe.transpose(ps[:, n * P:(n + 1) * P], ol[:, n * P:(n + 1) * P], ident[:])
                mm.then_inc(aux_filled, 1)

            def ot(step):
                u = step[1]
                ps = take_bank(step)
                pe.wait_ge(on_ready, u + 1)
                for qt in range(2):
                    mm = pe.transpose(ps[:, qt * P:(qt + 1) * P], on[:, qt, :], ident[:])
                mm.then_inc(aux_filled, 1)

            def ffn2(step):
                _, half, k, d = step
                m = hid_rows(k)
                if d == 0:
                    pe.wait_ge(g_lo, half * HT + k + 1)
                    if half == 0:
                        pe.wait_ge(w_lo, split_no[("ba", "w2", k)] + 1)
                        if k == 0:
                            pe.wait_ge(gate_done, 2 * HT)
                if k == 0 and half == 1:
                    pe.wait_ge(f_read, d + 1)
                w = [split_dst(("ba", "w2", k), part)[:, d * P:(d + 1) * P] for part in (0, 1)]
                mm = three_passes(bank[d][:, :], w, [g_entry(half, k, part) for part in (0, 1)],
                                  k == 0, k == HT - 1)
                if k == HT - 1:
                    mm.then_inc(f_ready, 1)
                elif d == DT - 1:
                    mm.then_inc(f_step, 1)

            def out_proj(step):
                _, half, d = step
                ps = take_bank(step)
                if d == 0:
                    pe.wait_ge(o_lo, 4 * (half + 1))
                    pe.wait_ge(w_lo, split_no[("w", "wo", 3)] + 1)
                for o in range(4):
                    mm = three_passes(ps[:, :], [stack[part][:, o, d * P:(d + 1) * P] for part in (0, 1)],
                                      [o_hi_tile(o), o_lo_tile(o)], o == 0, o == 3)
                mm.then_inc(aux_filled, 1)

            pe.wait_ge(const_in, 48)
            pe.wait_ge(lora_in, 96)
            do = {"xt": xt, "kv": kv, "vt": vt, "ba": ba, "q": q, "ffn1": ffn1, "max": causal_scores,
                  "mrow": max_rows, "exp": shifted_scores, "pv": pv, "olt": olt, "ot": ot,
                  "ffn2": ffn2, "wo": out_proj}
            for step in steps:
                if step[0] in do:
                    do[step[0]](step)

        @block.scalar
        def _(act):
            def split_weight(step):
                kind, name, i = step
                if kind == "ba":
                    act.wait_ge(merged, merged_no[step] + 1)
                else:
                    n = raw_no[step]
                    act.wait_ge(raw_in[n % RAW_RING], 16 * (n // RAW_RING + 1))
                if name == "w1" and i >= 2:
                    act.wait_ge(h_ready, 4 * (i - 2) + 3)
                if name == "w3" and i >= 2:
                    act.wait_ge(h_ready, 4 * (i - 2) + 4)
                if name == "w2" and i == 0:
                    wait_filled(act, ("q", UNITS // 2 - 1))
                if name == "w2" and i == 4:
                    act.wait_ge(h_ready, 4 * HT)
                if name == "wo" and i == 0:
                    wait_filled(act, ("exp", UNITS - 1, 5))
                nc.scalar.copy(split_dst(step, 0), split_src(step)).then_inc(w_hi, 1)

            for step in steps:
                kind = step[0]
                if kind == "ln":
                    act.wait_ge(var_ready, step[1] + 1)
                    h = step[1]
                    nc.scalar.activation(lnv[:, 1, 4 * h:4 * h + 4], lnv[:, 0, 4 * h:4 * h + 4],
                                         ACT.Sqrt).then_inc(std_ready, 1)
                elif kind in ("w", "ba"):
                    split_weight(step)
                elif kind == "xt":
                    i = step[1]
                    wait_filled(act, step)
                    nc.scalar.copy(xsplit[:, 0, :, i * P:(i + 1) * P],
                                   aux(step)[:].rearrange("p (c t) -> p c t", c=DT)).then_inc(xhi_ready, 1)
                elif kind == "kv":
                    half = step[1]
                    wait_filled(act, step)
                    nc.scalar.copy(kv_rows[:, half * HALF:(half + 1) * HALF],
                                   aux(step)[0:KV_ROWS, :]).then_inc(kv_copied, 1)
                elif kind == "q":
                    k = step[1]
                    wait_filled(act, step)
                    if k >= 2:
                        act.wait_ge(q_moved[k % 2], 16 * Q_DMAS * (k // 2))
                    nc.scalar.copy(qsplit[:, k % 2, 0, :], aux(step)[:]).then_inc(q_hi, 1)
                elif kind == "ffn1":
                    _, t, i = step
                    if i % 8 == 3:
                        half = i // 8
                        m = hid_rows(t)
                        act.wait_ge(h_ready, 4 * t + 2 * half + 1)
                        nc.scalar.activation(u_t[0:m, half, :], bank[2 * half][0:m, :], ACT.Tanh,
                                             scale=0.5).then_inc(tanh_done, 1)
                elif kind == "mrow":
                    _, u, qt = step
                    b2 = u % 2
                    wait_filled(act, step)
                    nc.scalar.copy(stack[(u // 2) % 2][96:100, :, b2 * SEQ + qt * P:b2 * SEQ + (qt + 1) * P],
                                   aux(step)[0:4, :].rearrange("p (j t) -> p j t", j=4)
                                   ).then_inc(mrow_ready, 1)
                elif kind == "exp":
                    _, u, k = step
                    wait_filled(act, step)
                    if k == 0 and u >= 1:
                        wait_filled(act, ("pv", u - 1))
                    if k < 2:
                        out = p1[:, k].rearrange("p j q -> p (j q)")
                    else:
                        out = p0[:, (k - 2) // 2, (k - 2) % 2].rearrange("p j q -> p (j q)")
                    nc.scalar.activation(out, aux(step)[:], ACT.Exp, scale=SCORE_SCALE
                                         ).then_inc(exp_done, 1)
                elif kind == "pv":
                    u = step[1]
                    wait_filled(act, step)
                    if u >= 1:
                        wait_filled(act, ("olt", u - 1))
                    nc.scalar.copy(ol[:], aux(step)[:]).then_inc(ol_ready, 1)
                elif kind == "ot":
                    half, o, b2 = unit(step[1])
                    t0 = (2 * half + b2) * SEQ
                    wait_filled(act, step)
                    nc.scalar.copy(oT[:, o, t0:t0 + SEQ], aux(step)[:, 0:SEQ]
                                   ).then_inc(oT_ready, 1)
                elif kind == "gsplit":
                    _, half, k = step
                    n = half * HT + k
                    act.wait_ge(gate_done, 2 * k + half + 1)
                    if n < 4:
                        act.wait_ge(h_ready, 4 * (HT - 1) if n < 2 else 4 * HT)
                    elif n - 4 < HT - 1:
                        act.wait_ge(f_step, n - 4 + 1)
                    elif n - 4 == HT - 1:
                        act.wait_ge(f_ready, DT)
                    else:
                        act.wait_ge(f_step, n - 4)
                    nc.scalar.copy(g_entry(half, k, 0), g_src(half, k)).then_inc(g_hi, 1)
                elif kind == "osplit":
                    _, half, o = step
                    act.wait_ge(oT_ready, UNITS if half else UNITS // 2)
                    if o == 0:
                        if half == 0:
                            wait_filled(act, ("exp", UNITS - 1, 5))
                        else:
                            wait_filled(act, ("wo", 0, DT - 1))
                    nc.scalar.copy(o_hi_tile(o), oT[:, o, half * HALF:(half + 1) * HALF]).then_inc(o_hi, 1)
                elif kind == "fin":
                    _, half, d = step
                    n = half * DT + d
                    act.wait_ge(f_ready, n + 1)
                    if n >= 2:
                        act.wait_ge(f_read, n - 1)
                    nc.scalar.activation(u_t[:, d % 2, :], bank[d][:], ACT.Tanh, scale=0.5).then_inc(ftanh, 1)

        @block.vector
        def _(dve):
            links = [0]

            def link(ins):
                links[0] += 1
                ins.then_inc(chain, 1)
                dve.wait_ge(chain, links[0])

            def layernorm(h):
                dve.wait_ge(x_in[h], 64)
                cols = slice(4 * h, 4 * h + 4)
                for i in range(4 * h, 4 * h + 4):
                    link(nc.vector.bn_stats(stats[:, i, :], x_tile(i)))
                    link(nc.vector.bn_aggr(mv[:, i, :], stats[:, i, :]))
                nc.vector.tensor_scalar(lnv[:, 0, cols], mv[:, cols, 1], LN_EPS, None,
                                        ALU.add).then_inc(var_ready, 1)
                dve.wait_ge(std_ready, h + 1)
                link(nc.vector.reciprocal(lnv[:, 2, cols], lnv[:, 1, cols]))
                link(nc.vector.tensor_tensor(lnv[:, 3, cols], lnv[:, 2, cols], lnv[:, 2, cols], ALU.mult))
                link(nc.vector.tensor_tensor(lnv[:, 3, cols], lnv[:, 3, cols], lnv[:, 0, cols], ALU.mult))
                link(nc.vector.tensor_scalar(lnv[:, 3, cols], lnv[:, 3, cols], -0.5, 1.5, ALU.mult, ALU.add))
                link(nc.vector.tensor_tensor(lnv[:, 4, cols], lnv[:, 2, cols], lnv[:, 3, cols], ALU.mult))
                for i in range(4 * h, 4 * h + 4):
                    nc.vector.tensor_scalar(xn_tile(i), x_tile(i), mv[:, i, 0:1], lnv[:, 4, i:i + 1],
                                            ALU.subtract, ALU.mult).then_inc(xn_ready, 1)

            def constants():
                dve.wait_ge(const_in, 48)
                nc.vector.tensor_copy(ident_b[:], ident[:])
                for n in range(4):
                    nc.vector.tensor_copy(mask_b[:, n, :], mask_f[:])
                link(nc.vector.memset(kst[96:P, :, :].bitcast(F32), 1.0))
                for e in range(2):
                    last = nc.vector.tensor_scalar(kst[96:P, e, :], kst[96:P, e, :].bitcast(F32),
                                                   sel[96:P, e:e + 1], None, ALU.mult)
                link(last)
                link(nc.vector.memset(vext[:], 0.0))
                nc.vector.memset(vext[:, :, HDIM:HDIM + 1], 1.0).then_inc(consts_ready, 1)

            for step in steps:
                kind = step[0]
                if kind == "ln":
                    layernorm(step[1])
                    if step[1] == 0:
                        constants()
                elif kind == "xt":
                    i = step[1]
                    wait_filled(dve, step)
                    dve.wait_ge(xhi_ready, i + 1)
                    nc.vector.tensor_tensor(xsplit[:, 1, :, i * P:(i + 1) * P],
                                            aux(step)[:].rearrange("p (c t) -> p c t", c=DT),
                                            xsplit[:, 0, :, i * P:(i + 1) * P].bitcast(F32),
                                            ALU.subtract).then_inc(xlo_ready, 1)
                elif kind == "kv":
                    half = step[1]
                    cols = slice(half * HALF, (half + 1) * HALF)
                    wait_filled(dve, step)
                    dve.wait_ge(kv_copied, half + 1)
                    for e in range(2):
                        last = nc.vector.tensor_scalar(kst[0:96, e, cols], aux(step)[0:96, :],
                                                       sel[0:96, e:e + 1], None, ALU.mult)
                    link(last)
                    for e in range(2):
                        last = nc.vector.scalar_tensor_tensor(
                            out=kst[64:96, e, cols], in0=aux(step)[64:96, :], scalar=sel[64:96, e:e + 1],
                            in1=kst[64:96, e, cols].bitcast(F32), op0=ALU.mult, op1=ALU.subtract)
                    last.then_inc(k_ready, 1)
                elif kind == "vt":
                    half = step[1]
                    wait_filled(dve, step)
                    nc.vector.tensor_copy(
                        vext[:, 4 * half:4 * half + 4, 0:HDIM],
                        aux(step)[:, 0:4 * KV_ROWS].rearrange("p (i r) -> p i r", i=4)[:, :, 96:KV_ROWS]
                    ).then_inc(v_ready, 1)
                elif kind == "ba":
                    _, name, i = step
                    n = raw_no[step]
                    wait_filled(dve, step)
                    dve.wait_ge(raw_in[n % RAW_RING], 16 * (n // RAW_RING + 1))
                    m = merged_no[step]
                    if m >= 2:
                        before = list(merged_no)[m - 2]
                        dve.wait_ge(w_lo, split_no[before] + 1)
                    rows = hid_rows(i) if name == "w2" else P
                    ps = aux(step)[0:rows] if name == "w2" else aux(step)[:]
                    nc.vector.scalar_tensor_tensor(
                        out=cut(weff[:, m % 2, :], name, i), in0=cut(ps, name, i), scalar=LORA_SCALE,
                        in1=cut(raw[:, n % RAW_RING, :], name, i), op0=ALU.mult, op1=ALU.add
                    ).then_inc(merged, 1)
                elif kind == "q":
                    k = step[1]
                    wait_filled(dve, step)
                    dve.wait_ge(q_hi, k + 1)
                    nc.vector.tensor_tensor(qsplit[:, k % 2, 1, :], aux(step)[:],
                                            qsplit[:, k % 2, 0, :].bitcast(F32),
                                            ALU.subtract).then_inc(q_lo, 1)
                elif kind == "ffn1":
                    _, t, i = step
                    if i % 8 == 7:
                        half = i // 8
                        m = hid_rows(t)
                        dve.wait_ge(tanh_done, 2 * t + half + 1)
                        link(nc.vector.scalar_tensor_tensor(
                            out=g1[0:m], in0=u_t[0:m, half, :], scalar=1.0, in1=bank[2 * half][0:m, :],
                            op0=ALU.add, op1=ALU.mult))
                        dve.wait_ge(h_ready, 4 * t + 2 * half + 2)
                        nc.vector.scalar_tensor_tensor(
                            out=g_src(half, t), in0=g1[0:m], scalar=0.5, in1=bank[2 * half + 1][0:m, :],
                            op0=ALU.mult, op1=ALU.mult).then_inc(gate_done, 1)
                elif kind == "max":
                    _, u, k = step
                    wait_filled(dve, step)
                    if k < 4:
                        out = negmax[:, 1, k, :]
                        src = aux(step)[:].rearrange("p (h k) -> p h k", h=2)
                    else:
                        out = negmax[:, 0, 2 * (k - 4):2 * (k - 4) + 2, :].rearrange("p j e -> p (j e)")
                        src = aux(step)[:].rearrange("p (h k) -> p h k", h=4)
                    ins = nc.vector.tensor_reduce(out, src, AX.X, ALU.max, negate=True)
                    ins.then_inc(max_done, 1)
                    if k == 5:
                        dve.wait_ge(max_done, 6 * u + 6)
                        if u >= 1:
                            wait_filled(dve, ("mrow", u - 1, 1))
                        nm = negmax[:].rearrange("p a j e -> p (a j) e")
                        ms = msplit[:].rearrange("p a j e -> p (a j) e")
                        link(nc.vector.tensor_copy(ms[:, :, 0:2], nm))
                        nc.vector.tensor_tensor(ms[:, :, 2:4], nm, ms[:, :, 0:2].bitcast(F32),
                                                ALU.subtract).then_inc(m_ready, 1)
                elif kind == "olt":
                    u = step[1]
                    wait_filled(dve, step)
                    if u >= 1:
                        wait_filled(dve, ("ot", u - 1))
                    v = aux(step)[:].rearrange("p (e a j c) -> p e a j c", e=2, a=2, j=4)
                    link(nc.vector.reciprocal(rden[:], v[:, :, :, :, HDIM]))
                    for qt in range(2):
                        last = nc.vector.tensor_tensor(
                            on[:, qt, :].rearrange("p (j e c) -> p e j c", j=4, e=2),
                            v[:, :, qt, :, 0:HDIM],
                            rden[:, :, qt, :].unsqueeze(3).to_broadcast([P, 2, 4, HDIM]), ALU.mult)
                    last.then_inc(on_ready, 1)
                elif kind == "gsplit":
                    _, half, k = step
                    dve.wait_ge(g_hi, half * HT + k + 1)
                    nc.vector.tensor_tensor(g_entry(half, k, 1), g_src(half, k),
                                            g_entry(half, k, 0).bitcast(F32), ALU.subtract).then_inc(g_lo, 1)
                elif kind == "fin":
                    _, half, d = step
                    n = half * DT + d
                    r = raw_no[step]
                    gate = g[:, d, half * HALF:(half + 1) * HALF]
                    dve.wait_ge(ftanh, n + 1)
                    ins = nc.vector.scalar_tensor_tensor(out=gate, in0=u_t[:, d % 2, :], scalar=1.0,
                                                         in1=bank[d][:], op0=ALU.add, op1=ALU.mult)
                    ins.then_inc(f_read, 1)
                    dve.wait_ge(f_read, n + 1)
                    wait_filled(dve, ("wo", half, d))
                    if half == 1:
                        dve.wait_ge(y_out[d], 16)
                    ins = nc.vector.scalar_tensor_tensor(out=y[:, d, :], in0=gate, scalar=0.5,
                                                         in1=aux(("wo", half, d))[:], op0=ALU.mult, op1=ALU.mult)
                    ins.then_inc(s_read, 1)
                    dve.wait_ge(s_read, n + 1)
                    dve.wait_ge(raw_in[r % RAW_RING], 16 * (r // RAW_RING + 1))
                    nc.vector.tensor_tensor(y[:, d, :], y[:, d, :], raw[:, r % RAW_RING, :],
                                            ALU.add).then_inc(y_ready, 1)

        @block.gpsimd
        def _(pool):
            for step in steps:
                kind = step[0]
                if kind in ("w", "ba"):
                    pool.wait_ge(w_hi, split_no[step] + 1)
                    nc.gpsimd.tensor_tensor(split_dst(step, 1), split_src(step),
                                            split_dst(step, 0).bitcast(F32), ALU.subtract).then_inc(w_lo, 1)
                elif kind == "exp" and step[2] % 2 == 1:
                    _, u, k = step
                    pool.wait_ge(exp_done, 6 * u + k + 1)
                    if k == 1:
                        v = p1[:].rearrange("p e j q -> p (e j) q")
                    else:
                        v = p0[:, (k - 2) // 2].rearrange("p e j q -> p (e j) q")[:, :, 0:P]
                    nh = 8 if k == 1 else 4
                    nc.gpsimd.affine_select(out=v, in_=v, compare_op=ALU.is_ge, fill=0.0, base=0,
                                            pattern=[[0, nh], [1, P]], channel_multiplier=-1
                                            ).then_inc(p_masked, 1)
                elif kind == "osplit":
                    _, half, o = step
                    pool.wait_ge(o_hi, 4 * half + o + 1)
                    nc.gpsimd.tensor_tensor(o_lo_tile(o), oT[:, o, half * HALF:(half + 1) * HALF],
                                            o_hi_tile(o).bitcast(F32), ALU.subtract).then_inc(o_lo, 1)


def kernel(L0_attn_x, L0_attn_wq, L0_attn_wk, L0_attn_wv, L0_attn_wo, L0_ffn_w1, L0_ffn_w3, L0_ffn_w2,
           L0_ffn_lora_A1, L0_ffn_lora_B1, L0_ffn_lora_A3, L0_ffn_lora_B3, L0_ffn_lora_A2, L0_ffn_lora_B2):
    import concourse.bacc as bacc
    from concourse.bass_utils import run_bass_kernel_spmd

    x = np.ascontiguousarray(L0_attn_x).reshape(TOK, DIM)
    main = (HT - 1) * P

    def tiles(w):
        wt = np.asarray(w).T
        n = wt.shape[1] // P
        whole = wt[:, :n * P].reshape(DT, P, n, P).transpose(2, 1, 0, 3).reshape(n, P, DT * P)
        last = wt[:, n * P:].reshape(DT, P, -1).transpose(1, 0, 2)
        return whole, last

    w1, w1_last = tiles(L0_ffn_w1)
    w3, w3_last = tiles(L0_ffn_w3)
    wq, _ = tiles(np.asarray(L0_attn_wq).T)
    wkv = np.concatenate([np.asarray(L0_attn_wk)] * 6 + [np.asarray(L0_attn_wv)], axis=1)
    wkv = wkv.reshape(DT, P, KV_ROWS).transpose(1, 0, 2).reshape(P, DT * KV_ROWS)
    consts = np.zeros((P, 2 * P + 2), np.float32)
    consts[:, 0:P] = np.eye(P)
    consts[:, P:2 * P] = np.where(np.arange(P)[None, :] > np.arange(P)[:, None], NEG, 0.0)
    for e in range(2):
        consts[0:96, 2 * P + e] = (np.arange(96) // HDIM) % 2 == e
        consts[96:100, 2 * P + e] = np.arange(4) % 2 == e
    arrays = {
        "x": x, "xT": x.T, "wq": wq, "wkv": wkv, "wo": L0_attn_wo, "w1": w1, "w1_last": w1_last,
        "w3": w3, "w3_last": w3_last, "w2T": np.asarray(L0_ffn_w2).T,
        "A1": L0_ffn_lora_A1, "A3": L0_ffn_lora_A3, "B2T": np.asarray(L0_ffn_lora_B2).T,
        "B1T": np.asarray(L0_ffn_lora_B1).T, "B3T": np.asarray(L0_ffn_lora_B3).T, "A2": L0_ffn_lora_A2,
        "consts": consts,
    }
    arrays = {f"in_{k}": np.ascontiguousarray(v) for k, v in arrays.items()}
    nc = bacc.Bacc("TRN2", target_bir_lowering=False, num_devices=1)
    ap = {k[3:]: nc.dram_tensor(k, v.shape, F32, kind="ExternalInput").ap() for k, v in arrays.items()}
    outT = nc.dram_tensor("outT", (DIM, TOK), F32, kind="ExternalOutput").ap()
    mixed_block_kernel(nc, ap["x"], ap["xT"], ap["wq"], ap["wkv"], ap["wo"], ap["w1"], ap["w1_last"],
                       ap["w3"], ap["w3_last"], ap["w2T"], [ap["A1"], ap["A3"], ap["B2T"]],
                       [ap["B1T"], ap["B3T"], ap["A2"]], ap["consts"], outT)
    r = run_bass_kernel_spmd(nc, [arrays], core_ids=[0])
    return np.ascontiguousarray(r.results[0]["outT"].T).reshape(BATCH, SEQ, DIM)
```

```python
from contextlib import ExitStack

import numpy as np

import concourse.bass as bass
from concourse import mybir

F32 = mybir.dt.float32
F32R = mybir.dt.float32r
ALU = mybir.AluOpType
ACT = mybir.ActivationFunctionType
AX = mybir.AxisListType

P = 128
BATCH, SEQ, DIM = 4, 256, 512
TOK = BATCH * SEQ
HALF = TOK // 2
HID, RANK = 1376, 16
HEADS, HDIM = 32, 16
DT = DIM // P
HT = -(-HID // P)
HLAST = HID - (HT - 1) * P
LORA_SCALE = 2.0
LN_EPS = 1e-5
SCORE_SCALE = float(HDIM) ** -0.5
NEG = -1.0e30
UNITS = BATCH * HEADS // 8
RAW_RING = 4
AUX0, AUX_RING = 4, 4
KV_ROWS = 6 * HDIM + HDIM
Q_DMAS = 12
M_DMAS = 4
LROWS = 3 * RANK
KROWS = 100


PER_SLOT = 10


def hid_rows(t):
    return P if t < HT - 1 else HLAST


def unit(u):
    return u // 8, (u % 8) // 2, u % 2


def plan():
    def hidden(n):
        t, i = n // 16, n % 16
        group = [("ffn1", t, i)]
        if t + 1 < HT:
            group += {3: [("ba", "w1", t + 1)], 7: [("ba", "w3", t + 1)]}.get(i, [])
        else:
            group += {1: [("ba", "w2", 0)], 4: [("ba", "w2", 1)], 7: [("ba", "w2", 2)],
                      10: [("ba", "w2", 3)], 12: [("gsplit", 0, 0)], 14: [("gsplit", 0, 1)]}.get(i, [])
        return group

    def down(half):
        for k in range(HT):
            ahead = []
            if half == 0 and k + 4 < HT:
                ahead.append(("ba", "w2", k + 4))
            n = half * HT + k + 2
            if n < 2 * HT:
                ahead.append(("gsplit", n // HT, n % HT))
            if half == 0 and k >= HT - 4:
                ahead += [("w", "wo", k - HT + 4), ("osplit", 0, k - HT + 4)]
            if half == 1 and 1 <= k < 5:
                ahead.append(("osplit", 1, k - 1))
            if half == 1 and 3 <= k < 7:
                ahead.append(("wo", 1, k - 3))
            if half == 0 and k < 2:
                order = [(0, 0), (0, 1)] if k == 0 else [(1, 0), (1, 1), (0, 2), (0, 3), (1, 2), (1, 3)]
            elif half == 0 or k < HT - 4:
                order = [(k, d) for d in range(DT)]
            else:
                order = []
            yield ahead
            for kk, d in order:
                yield [("ffn2", half, kk, d)]
        if half == 1:
            for d in range(DT):
                yield [("ffn2", 1, k, d) for k in range(HT - 4, HT)] + [("fin", 1, d)]

    steps = [("ln", 0), ("ln", 1), ("w", "wkv", 0), ("xt", 0), ("xt", 1), ("w", "wq", 0), ("xt", 2),
             ("xt", 3), ("lora", 0, 0), ("lora", 1, 0), ("kv", 0), ("ba", "w1", 0), ("q", 0),
             ("ba", "w3", 0), ("ln", 2)]
    for n in range(8):
        steps += hidden(n)
        steps += {0: [("xt", 4), ("xt", 5)], 1: [("ln", 3)], 4: [("xt", 6)], 5: [("xt", 7)],
                  6: [("lora", 0, 1), ("lora", 1, 1)]}.get(n, [])
    steps += [("kv", 1), ("vt", 0), ("vt", 1)]
    main = [hidden(n) for n in range(8, 16 * HT)] + [x for x in down(0) if x]
    at = 0
    for s in range(UNITS + 2):
        a, b, c = s, s - 1, s - 2
        for k in range(PER_SLOT):
            steps += main[at]
            at += 1
            if a < UNITS:
                steps += {0: [("max", a, 0)], 1: [("max", a, 1)], 2: [("max", a, 2)],
                          3: [("max", a, 3)], 4: [("max", a, 4)], 5: [("max", a, 5)],
                          7: [("mrow", a)]}.get(k, [])
            if 0 <= c < UNITS:
                steps += {1: [("pv", c)], 4: [("olt", c)], 8: [("ot", c)]}.get(k, [])
            if 0 <= b < UNITS:
                steps += {2: [("exp", b, 0)], 3: [("exp", b, 1)], 4: [("exp", b, 2)],
                          5: [("exp", b, 3)], 6: [("exp", b, 4)], 7: [("exp", b, 5)]}.get(k, [])
            if s % 2 == 0 and s // 2 + 1 < UNITS // 2:
                if k == 2 and s // 2 + 1 < 4:
                    steps.append(("w", "wq", s // 2 + 1))
                if k == 8:
                    steps.append(("q", s // 2 + 1))
            if s == 0 and k == 5:
                steps.append(("lora", 2, 0))
    for group in main[at:]:
        steps += group
    steps += [("wo", 0, d) for d in range(DT)] + [("fin", 0, d) for d in range(DT)]
    for group in down(1):
        steps += group
    return steps


AUX_JOBS = {"xt", "kv", "vt", "ba", "q", "max", "mrow", "exp", "pv", "olt", "ot", "wo"}


def number(steps, kinds):
    return {s: n for n, s in enumerate(s for s in steps if s[0] in kinds)}


def mixed_block_kernel(nc, x, xT, wq, wkv, wo, w1, w1_last, w3, w3_last, w2T,
                       first_in, second_in, consts, outT):
    steps = plan()
    aux_no = number(steps, AUX_JOBS)
    aux_steps = list(aux_no)
    split_no = number(steps, {"w", "ba"})
    merged_no = number(steps, {"ba"})
    raw_steps = [s for s in steps if s[0] in ("w", "ba", "fin")]
    raw_no = {s: n for n, s in enumerate(raw_steps)}
    lora_steps = [s for s in steps if s[0] == "lora"]

    with ExitStack() as ctx:
        def sb(name, shape, dt=F32):
            return ctx.enter_context(nc.sbuf_tensor(name, shape, dt))

        def sem(name):
            return ctx.enter_context(nc.semaphore(name))

        bank = [ctx.enter_context(nc.psum_tensor(f"bank{i}", [P, 512], F32)) for i in range(8)]

        ident = sb("ident", [P, P])
        mask = sb("mask", [P, 2 * P])
        sel = sb("sel", [P, 2])
        lora_b = sb("lora_b", [P, HID], F32R)
        lora_a = sb("lora_a", [P, DIM], F32R)
        lora_a2 = sb("lora_a2", [LROWS, HID], F32R)
        lora_b2 = sb("lora_b2", [LROWS, DIM], F32R)
        raw = sb("raw", [P, RAW_RING, 512])
        weff = sb("weff", [P, 2, 512])
        xsplit = sb("xsplit", [P, 2, DT, TOK], F32R)
        wq_s = sb("wq_s", [P, 4, 2, 512], F32R)
        w13 = sb("w13", [P, 2, 2, 2, 512], F32R)
        g = sb("g", [P, HT, TOK])
        u_t = sb("u_t", [P, 2, 512])
        qsplit = sb("qsplit", [P, 2, 2, 512], F32R)
        stack = [sb(f"stack{i}", [P, 4, 512], F32R) for i in range(2)]
        wkv_s = stack[1][:, 0:2, 0:DT * KV_ROWS].rearrange("p s (c m) -> p s c m", c=DT)
        kst = sb("kst", [P, 2, TOK], F32R)
        vext = sb("vext", [P, 8, 32])
        rowmax = sb("rowmax", [P, 2, 4, 2])
        mrow = sb("mrow", [16, SEQ])
        msplit = sb("msplit", [P, 2, 4, 4], F32R)
        p0 = sb("p0", [P, 2, 2, 2, SEQ])
        p1 = sb("p1", [P, 2, 4, P])
        ol = sb("ol", [P, 512])
        rden = sb("rden", [P, 2, 2, 4])
        on = sb("on", [P, 2, P])
        oT = sb("oT", [P, 4, TOK])
        stats = sb("stats", [P, 8, 6])
        mv = sb("mv", [P, 8, 2])
        lnv = sb("lnv", [P, 6, 8])
        warm = sb("warm", [P, 2])
        y = p0[:].rearrange("p a e b q -> p (a e b q)").rearrange("p (n t) -> p n t", n=4)

        const_in = sem("const_in")
        lora_in = [sem(f"lora_in{r}") for r in range(3)]
        x_in = [sem(f"x_in{h}") for h in range(4)]
        raw_in = [sem(f"raw_in{i}") for i in range(RAW_RING)]
        q_moved = [sem(f"q_moved{i}") for i in range(2)]
        y_out = [sem(f"y_out{i}") for i in range(4)]
        aux_filled = sem("aux_filled")
        warm_ready = sem("warm_ready")
        lora_hi = sem("lora_hi")
        lora_lo = sem("lora_lo")
        lora_ready = sem("lora_ready")
        m_moved = sem("m_moved")
        var_ready = sem("var_ready")
        std_ready = sem("std_ready")
        xn_ready = sem("xn_ready")
        xhi_ready = sem("xhi_ready")
        xlo_ready = sem("xlo_ready")
        kv_copied = sem("kv_copied")
        k_ready = sem("k_ready")
        v_ready = sem("v_ready")
        merged = sem("merged")
        max_done = sem("max_done")
        s_read = sem("s_read")
        w_hi = sem("w_hi")
        w_lo = sem("w_lo")
        h_ready = sem("h_ready")
        tanh_done = sem("tanh_done")
        gate_done = sem("gate_done")
        q_hi = sem("q_hi")
        q_lo = sem("q_lo")
        m_ready = sem("m_ready")
        mrow_ready = sem("mrow_ready")
        exp_done = sem("exp_done")
        p_masked = sem("p_masked")
        ol_ready = sem("ol_ready")
        on_ready = sem("on_ready")
        oT_ready = sem("oT_ready")
        g_hi = sem("g_hi")
        g_lo = sem("g_lo")
        o_hi = sem("o_hi")
        o_lo = sem("o_lo")
        f_step = sem("f_step")
        f_ready = sem("f_ready")
        ftanh = sem("ftanh")
        f_read = sem("f_read")
        y_ready = sem("y_ready")
        chain = sem("chain")

        def x_tile(i):
            return g[:, 7 + i // 2, (i % 2) * 512:(i % 2) * 512 + 512]

        def xn_tile(i):
            return g[:, 3 + i // 2, (i % 2) * 512:(i % 2) * 512 + 512]

        kv_rows = g[0:KV_ROWS, 2, :]
        oT_flat = oT[:].rearrange("p o t -> p (o t)")
        def lora_cols(r, part):
            if r == 2:
                return slice(0, DIM)
            return slice(0, 2 * P) if part == 0 else slice(2 * P, HID)

        def lora_raw(rows, column, n):
            return oT_flat[rows, column:column + n]

        lower, upper = slice(0, LROWS), slice(64, 64 + LROWS)
        lora_first = [(lora_a[lower, :], lora_raw(lower, HID, DIM)),
                      (lora_a[upper, :], lora_raw(upper, HID, DIM)),
                      (lora_a2[:], lora_raw(lower, HID + DIM, HID))]
        lora_second = [(lora_b[lower, :], lora_raw(lower, 0, HID)),
                       (lora_b[upper, :], lora_raw(upper, 0, HID)),
                       (lora_b2[:], lora_raw(lower, 2 * HID + DIM, DIM))]

        def wait_read(eng, step):
            kind, *at = step
            last_reader = {
                "xt": lambda i: (xlo_ready, i + 1),
                "kv": lambda half: (k_ready, half + 1),
                "vt": lambda half: (v_ready, half + 1),
                "ba": lambda name, i: (merged, merged_no[step] + 1),
                "q": lambda k: (q_lo, k + 1),
                "max": lambda u, k: (max_done, 6 * u + k + 1),
                "mrow": lambda u: (mrow_ready, u + 1),
                "exp": lambda u, k: (exp_done, 6 * u + k + 1),
                "pv": lambda u: (ol_ready, u + 1),
                "olt": lambda u: (on_ready, u + 1),
                "ot": lambda u: (oT_ready, u + 1),
                "wo": lambda half, d: (s_read, DT * half + d + 1),
            }
            eng.wait_ge(*last_reader[kind](*at))

        def wait_filled(eng, step):
            eng.wait_ge(aux_filled, aux_no[step] + 1)

        def aux(step):
            return bank[AUX0 + aux_no[step] % AUX_RING]

        def split_dst(step, part):
            _, name, i = step
            if name == "wkv":
                return wkv_s[:, part]
            if name == "wq":
                return wq_s[:, i, part, :]
            if name == "wo":
                return stack[part][:, i, :]
            if name == "w2":
                if i < 4:
                    return wq_s[0:hid_rows(i), i, part, :]
                j = i - 4
                return xsplit[0:hid_rows(i), part, j // 2, (j % 2) * 512:(j % 2) * 512 + 512]
            m = hid_rows(i)
            tile = w13[:, i % 2, 0 if name == "w1" else 1, part, :]
            return tile.rearrange("p (c m) -> p c m", c=DT)[:, :, 0:m]

        def split_src(step):
            kind, name, i = step
            if kind == "ba":
                tile = weff[:, merged_no[step] % 2, :]
            else:
                tile = raw[:, raw_no[step] % RAW_RING, :]
            if name == "wkv":
                return tile[:, 0:DT * KV_ROWS].rearrange("p (c m) -> p c m", c=DT)
            if name in ("wq", "wo"):
                return tile
            return cut(tile, name, i)

        def cut(tile, name, i):
            if name == "w2":
                return tile[0:hid_rows(i)]
            return tile.rearrange("p (c m) -> p c m", c=DT)[:, :, 0:hid_rows(i)]

        def g_entry(half, k, part):
            n = (half * HT + k) % 4
            return w13[0:hid_rows(k), (n // 2 + 1) % 2, n % 2, part, :]

        def g_src(half, k):
            return g[0:hid_rows(k), k, half * HALF:(half + 1) * HALF]

        def o_hi_tile(o):
            return kst[:, o // 2, (o % 2) * 512:(o % 2) * 512 + 512]

        def o_lo_tile(o):
            return qsplit[:, o // 2, o % 2, :]

        block = ctx.enter_context(nc.Block())

        @block.sync
        def _(sp):
            def load_x(h):
                for i in (2 * h, 2 * h + 1):
                    sp.dma_start(x_tile(i), x[i * P:(i + 1) * P, :]).then_inc(x_in[h], 16)

            load_x(0)
            sp.dma_start(ident[:], consts[:, 0:P]).then_inc(const_in, 16)
            sp.dma_start(mask[:], consts[:, P:3 * P]).then_inc(const_in, 16)
            sp.dma_start(sel[:], consts[:, 3 * P:3 * P + 2]).then_inc(const_in, 16)
            load_x(1)

            def load_raw(step):
                n = raw_no[step]
                if n >= RAW_RING:
                    old = raw_steps[n - RAW_RING]
                    if old[0] == "w":
                        sp.wait_ge(w_lo, split_no[old] + 1)
                    elif old[0] == "ba":
                        sp.wait_ge(merged, merged_no[old] + 1)
                    else:
                        sp.wait_ge(y_ready, old[1] * DT + old[2] + 1)
                kind, name, i = step
                tile = raw[:, n % RAW_RING, :]
                if kind == "fin":
                    half, d = name, i
                    src = xT[d * P:(d + 1) * P, half * HALF:(half + 1) * HALF]
                    dst = tile
                elif name == "wkv":
                    src, dst = wkv, tile[:, 0:DT * KV_ROWS]
                elif name == "wq":
                    src, dst = wq[i], tile
                elif name == "wo":
                    src, dst = wo[i * P:(i + 1) * P, :], tile
                elif name == "w2":
                    src, dst = w2T[i * P:i * P + hid_rows(i), :], tile[0:hid_rows(i)]
                else:
                    main, last = (w1, w1_last) if name == "w1" else (w3, w3_last)
                    if i < HT - 1:
                        src, dst = main[i], tile
                    else:
                        src, dst = last, cut(tile, name, i)
                sp.dma_start(dst, src).then_inc(raw_in[n % RAW_RING], 16)

            def move_queries(k):
                sp.wait_ge(q_lo, k + 1)
                if k >= 2:
                    wait_filled(sp, ("exp", 2 * (k - 2) + 1, 5))
                for blk, part in enumerate((0, 1, 0)):
                    for j in range(4):
                        sp.dma_start(stack[k % 2][32 * blk:32 * blk + 32, j, :].bitcast(F32),
                                     qsplit[32 * j:32 * j + 32, k % 2, part, :].bitcast(F32)
                                     ).then_inc(q_moved[k % 2], 16)

            def move_maxima(u):
                b2 = u % 2
                sp.wait_ge(mrow_ready, u + 1)
                for j in range(4):
                    sp.dma_start(stack[(u // 2) % 2][96:100, j, b2 * SEQ:(b2 + 1) * SEQ].bitcast(F32),
                                 mrow[4 * j:4 * j + 4, :]).then_inc(m_moved, 16)

            def load_lora(r):
                sp.dma_start(lora_first[r][1], first_in[r]).then_inc(lora_in[r], 16)
                sp.dma_start(lora_second[r][1], second_in[r]).then_inc(lora_in[r], 16)

            load_raw(raw_steps[0])
            load_raw(raw_steps[1])
            load_lora(0)
            load_lora(1)
            load_raw(raw_steps[2])
            load_raw(raw_steps[3])
            load_x(2)
            load_x(3)
            load_lora(2)
            for step in steps:
                if step in raw_no and raw_no[step] + RAW_RING < len(raw_steps):
                    load_raw(raw_steps[raw_no[step] + RAW_RING])
                if step[0] == "q":
                    move_queries(step[1])
                if step[0] == "mrow":
                    move_maxima(step[1])
                if step[0] == "fin":
                    _, half, d = step
                    sp.wait_ge(y_ready, half * DT + d + 1)
                    sp.dma_start(outT[d * P:(d + 1) * P, half * HALF:(half + 1) * HALF],
                                 y[:, d, :]).then_inc(y_out[d], 16)
            for d in range(DT):
                sp.wait_ge(y_out[d], 32)

        @block.tensor
        def _(pe):
            def take_bank(step):
                n = aux_no[step]
                if n >= AUX_RING:
                    wait_read(pe, aux_steps[n - AUX_RING])
                return aux(step)

            def three_passes(out, w_parts, m_parts, start, stop):
                pe.matmul(out, w_parts[0], m_parts[0], start=start, stop=False)
                pe.matmul(out, w_parts[0], m_parts[1], start=False, stop=False)
                return pe.matmul(out, w_parts[1], m_parts[0], start=False, stop=stop)

            def x_parts(c, half):
                return [xsplit[:, part, c, half * HALF:(half + 1) * HALF] for part in (0, 1)]

            def xt(step):
                i = step[1]
                ps = take_bank(step)
                pe.wait_ge(xn_ready, i + 1)
                for c in range(DT):
                    mm = pe.transpose(ps[:, c * P:(c + 1) * P], xn_tile(i)[:, c * P:(c + 1) * P], ident[:])
                mm.then_inc(aux_filled, 1)

            def kv(step):
                half = step[1]
                ps = take_bank(step)
                pe.wait_ge(w_lo, split_no[("w", "wkv", 0)] + 1)
                pe.wait_ge(xlo_ready, 4 * (half + 1))
                for c in range(DT):
                    mm = three_passes(ps[0:KV_ROWS, :], [wkv_s[:, part, c, :] for part in (0, 1)],
                                      x_parts(c, half), c == 0, c == DT - 1)
                mm.then_inc(aux_filled, 1)

            def vt(step):
                half = step[1]
                ps = take_bank(step)
                pe.wait_ge(kv_copied, half + 1)
                for i in range(4):
                    t0 = half * HALF + i * P
                    mm = pe.transpose(ps[:, i * KV_ROWS:(i + 1) * KV_ROWS], kv_rows[:, t0:t0 + P],
                                      ident[0:KV_ROWS, 0:KV_ROWS])
                mm.then_inc(aux_filled, 1)

            def ba(step):
                _, name, i = step
                ps = take_bank(step)
                m = hid_rows(i)
                r = {"w1": 0, "w3": 1, "w2": 2}[name]
                first, second = lora_first[r][0], lora_second[r][0]
                if name == "w2":
                    pe.wait_ge(lora_ready, len(lora_steps))
                else:
                    pe.wait_ge(lora_ready, lora_steps.index(("lora", r, 0 if i < 2 else 1)) + 1)
                if name == "w2":
                    mm = pe.matmul(ps[0:m, :], first[:, i * P:i * P + m], second, start=True, stop=True)
                else:
                    for c in range(DT):
                        mm = pe.matmul(ps[:, c * P:c * P + m], first[:, c * P:(c + 1) * P],
                                       second[:, i * P:i * P + m], start=True, stop=True)
                mm.then_inc(aux_filled, 1)

            def q(step):
                half, o, _ = unit(2 * step[1])
                ps = take_bank(step)
                pe.wait_ge(w_lo, split_no[("w", "wq", o)] + 1)
                for c in range(DT):
                    mm = three_passes(ps[:, :], [wq_s[:, o, part, c * P:(c + 1) * P] for part in (0, 1)],
                                      x_parts(c, half), c == 0, c == DT - 1)
                mm.then_inc(aux_filled, 1)

            def ffn1(step):
                _, t, i = step
                half, w, c = i // 8, (i // 4) % 2, i % 4
                m = hid_rows(t)
                if i == 0:
                    pe.wait_ge(w_lo, split_no[("ba", "w1", t)] + 1)
                if i == 4:
                    pe.wait_ge(w_lo, split_no[("ba", "w3", t)] + 1)
                if t == 0 and i % 8 == 0:
                    pe.wait_ge(xlo_ready, 4 * (half + 1))
                if c == 0 and t >= 1:
                    pe.wait_ge(gate_done, 2 * (t - 1) + half + 1)
                ps = bank[2 * half + w]
                mm = three_passes(ps[0:m, :], [w13[:, t % 2, w, part, c * P:c * P + m] for part in (0, 1)],
                                  x_parts(c, half), c == 0, c == DT - 1)
                if c == DT - 1:
                    mm.then_inc(h_ready, 1)

            def causal_scores(step):
                _, u, k = step
                half, o, b2 = unit(u)
                kcol = (2 * half + b2) * SEQ
                st = stack[(u // 2) % 2]
                ps = take_bank(step)
                if k == 0:
                    pe.wait_ge(q_moved[(u // 2) % 2], 16 * Q_DMAS * (u // 4 + 1))
                    if u == 0:
                        pe.wait_ge(k_ready, 2)
                if k < 4:
                    mm = pe.matmul(ps[:, :], st[0:96, k, b2 * SEQ + P:b2 * SEQ + 2 * P],
                                   kst[0:96, :, kcol:kcol + SEQ], start=True, stop=True)
                else:
                    for n in range(2):
                        mm = pe.matmul(ps[:, 256 * n:256 * n + 256],
                                       st[0:96, 2 * (k - 4) + n, b2 * SEQ:b2 * SEQ + P],
                                       kst[0:96, :, kcol:kcol + P], start=True, stop=True)
                mm.then_inc(aux_filled, 1)

            def max_rows(step):
                u = step[1]
                ps = take_bank(step)
                pe.wait_ge(m_ready, u + 1)
                for qt in range(2):
                    mm = pe.transpose(ps[0:16, qt * P:(qt + 1) * P],
                                      msplit[:, qt].rearrange("p j r -> p (j r)").bitcast(F32), ident[:])
                mm.then_inc(aux_filled, 1)

            def shifted_scores(step):
                _, u, k = step
                half, o, b2 = unit(u)
                kcol = (2 * half + b2) * SEQ
                st = stack[(u // 2) % 2]
                ps = take_bank(step)
                if k == 0:
                    pe.wait_ge(m_moved, 16 * M_DMAS * (u + 1))
                if k < 2:
                    mm = pe.matmul(ps[:, :], kst[0:KROWS, k, kcol + P:kcol + 2 * P],
                                   st[0:KROWS, :, b2 * SEQ + P:b2 * SEQ + 2 * P], start=True, stop=True)
                else:
                    pp, e = (k - 2) // 2, (k - 2) % 2
                    mm = pe.matmul(ps[:, :], kst[0:KROWS, e, kcol:kcol + P],
                                   st[0:KROWS, 2 * pp:2 * pp + 2, b2 * SEQ:(b2 + 1) * SEQ],
                                   start=True, stop=True)
                mm.then_inc(aux_filled, 1)

            def pv(step):
                u = step[1]
                half, o, b2 = unit(u)
                kt = 2 * (2 * half + b2)
                ps = take_bank(step)
                if u == 0:
                    pe.wait_ge(v_ready, 2)
                pe.wait_ge(p_masked, 3 * (u + 1))
                for j in range(4):
                    pe.matmul(ps[32 * j:32 * j + 32, :], vext[:, kt, :], p0[:, j // 2, :, j % 2, :],
                              start=True, stop=False)
                for j in range(4):
                    out = ps[32 * j:32 * j + 32, :].rearrange("p (e q) -> p e q", e=2)[:, :, P:2 * P]
                    mm = pe.matmul(out, vext[:, kt + 1, :], p1[:, :, j, :], start=False, stop=True)
                mm.then_inc(aux_filled, 1)

            def olt(step):
                u = step[1]
                ps = take_bank(step)
                pe.wait_ge(ol_ready, u + 1)
                for n in range(4):
                    mm = pe.transpose(ps[:, n * P:(n + 1) * P], ol[:, n * P:(n + 1) * P], ident[:])
                mm.then_inc(aux_filled, 1)

            def ot(step):
                u = step[1]
                ps = take_bank(step)
                pe.wait_ge(on_ready, u + 1)
                for qt in range(2):
                    mm = pe.transpose(ps[:, qt * P:(qt + 1) * P], on[:, qt, :], ident[:])
                mm.then_inc(aux_filled, 1)

            def ffn2(step):
                _, half, k, d = step
                m = hid_rows(k)
                if half == 0 and k == 0 and d % 2 == 0:
                    pe.wait_ge(gate_done, 2 * HT - 1 + d // 2)
                if d == 0:
                    pe.wait_ge(g_lo, half * HT + k + 1)
                    if half == 0:
                        pe.wait_ge(w_lo, split_no[("ba", "w2", k)] + 1)
                if k == 0 and half == 1:
                    pe.wait_ge(f_read, d + 1)
                w = [split_dst(("ba", "w2", k), part)[:, d * P:(d + 1) * P] for part in (0, 1)]
                mm = three_passes(bank[d][:, :], w, [g_entry(half, k, part) for part in (0, 1)],
                                  k == 0, k == HT - 1)
                if k == HT - 1:
                    mm.then_inc(f_ready, 1)
                elif d == DT - 1:
                    mm.then_inc(f_step, 1)

            def out_proj(step):
                _, half, d = step
                ps = take_bank(step)
                if d == 0:
                    pe.wait_ge(o_lo, 4 * (half + 1))
                    pe.wait_ge(w_lo, split_no[("w", "wo", 3)] + 1)
                for o in range(4):
                    mm = three_passes(ps[:, :], [stack[part][:, o, d * P:(d + 1) * P] for part in (0, 1)],
                                      [o_hi_tile(o), o_lo_tile(o)], o == 0, o == 3)
                mm.then_inc(aux_filled, 1)

            pe.wait_ge(const_in, 48)
            do = {"xt": xt, "kv": kv, "vt": vt, "ba": ba, "q": q, "ffn1": ffn1, "max": causal_scores,
                  "mrow": max_rows, "exp": shifted_scores, "pv": pv, "olt": olt, "ot": ot,
                  "ffn2": ffn2, "wo": out_proj}
            for step in steps:
                if step[0] in do:
                    do[step[0]](step)

        @block.scalar
        def _(act):
            def split_weight(step):
                kind, name, i = step
                if kind == "ba":
                    act.wait_ge(merged, merged_no[step] + 1)
                else:
                    n = raw_no[step]
                    act.wait_ge(raw_in[n % RAW_RING], 16 * (n // RAW_RING + 1))
                if name == "w1" and i >= 2:
                    act.wait_ge(h_ready, 4 * (i - 2) + 3)
                if name == "w3" and i >= 2:
                    act.wait_ge(h_ready, 4 * (i - 2) + 4)
                if name == "w2" and i == 0:
                    wait_filled(act, ("q", UNITS // 2 - 1))
                if name == "w2" and i == 4:
                    act.wait_ge(h_ready, 4 * HT)
                if name == "wo" and i == 0:
                    wait_filled(act, ("exp", UNITS - 1, 5))
                nc.scalar.copy(split_dst(step, 0), split_src(step)).then_inc(w_hi, 1)

            def split_lora(step):
                _, r, part = step
                cols = lora_cols(r, part)
                act.wait_ge(lora_in[r], 32)
                nc.scalar.copy(lora_second[r][0][:, cols], lora_second[r][1][:, cols]).then_inc(lora_hi, 1)
                if part == 0:
                    nc.scalar.copy(lora_first[r][0], lora_first[r][1]).then_inc(lora_hi, 1)

            act.wait_ge(warm_ready, 1)
            nc.scalar.activation(warm[:, 1:2], warm[:, 0:1], ACT.Sqrt)
            for step in steps:
                kind = step[0]
                if kind == "lora":
                    split_lora(step)
                elif kind == "ln":
                    h = step[1]
                    act.wait_ge(var_ready, h + 1)
                    nc.scalar.activation(lnv[:, 1, 2 * h:2 * h + 2], lnv[:, 0, 2 * h:2 * h + 2],
                                         ACT.Sqrt).then_inc(std_ready, 1)
                elif kind in ("w", "ba"):
                    split_weight(step)
                elif kind == "xt":
                    i = step[1]
                    wait_filled(act, step)
                    nc.scalar.copy(xsplit[:, 0, :, i * P:(i + 1) * P],
                                   aux(step)[:].rearrange("p (c t) -> p c t", c=DT)).then_inc(xhi_ready, 1)
                elif kind == "kv":
                    half = step[1]
                    wait_filled(act, step)
                    nc.scalar.copy(kv_rows[:, half * HALF:(half + 1) * HALF],
                                   aux(step)[0:KV_ROWS, :]).then_inc(kv_copied, 1)
                elif kind == "q":
                    k = step[1]
                    wait_filled(act, step)
                    if k >= 2:
                        act.wait_ge(q_moved[k % 2], 16 * Q_DMAS * (k // 2))
                    nc.scalar.copy(qsplit[:, k % 2, 0, :], aux(step)[:]).then_inc(q_hi, 1)
                elif kind == "ffn1":
                    _, t, i = step
                    if i % 8 == 3:
                        half = i // 8
                        m = hid_rows(t)
                        act.wait_ge(h_ready, 4 * t + 2 * half + 1)
                        nc.scalar.activation(u_t[0:m, half, :], bank[2 * half][0:m, :], ACT.Tanh,
                                             scale=0.5).then_inc(tanh_done, 1)
                elif kind == "mrow":
                    u = step[1]
                    wait_filled(act, step)
                    if u >= 1:
                        act.wait_ge(m_moved, 16 * M_DMAS * u)
                    nc.scalar.copy(mrow[:], aux(step)[0:16, 0:SEQ]).then_inc(mrow_ready, 1)
                elif kind == "exp":
                    _, u, k = step
                    wait_filled(act, step)
                    if k == 0 and u >= 1:
                        wait_filled(act, ("pv", u - 1))
                    if k < 2:
                        out = p1[:, k].rearrange("p j q -> p (j q)")
                    else:
                        out = p0[:, (k - 2) // 2, (k - 2) % 2].rearrange("p j q -> p (j q)")
                    nc.scalar.activation(out, aux(step)[:], ACT.Exp, scale=SCORE_SCALE
                                         ).then_inc(exp_done, 1)
                elif kind == "pv":
                    u = step[1]
                    wait_filled(act, step)
                    if u >= 1:
                        wait_filled(act, ("olt", u - 1))
                    nc.scalar.copy(ol[:], aux(step)[:]).then_inc(ol_ready, 1)
                elif kind == "ot":
                    half, o, b2 = unit(step[1])
                    t0 = (2 * half + b2) * SEQ
                    wait_filled(act, step)
                    nc.scalar.copy(oT[:, o, t0:t0 + SEQ], aux(step)[:, 0:SEQ]
                                   ).then_inc(oT_ready, 1)
                elif kind == "gsplit":
                    _, half, k = step
                    n = half * HT + k
                    act.wait_ge(gate_done, 2 * k + half + 1)
                    if n < 4:
                        act.wait_ge(h_ready, 4 * (HT - 1) if n < 2 else 4 * HT)
                    elif n - 4 < HT - 1:
                        act.wait_ge(f_step, n - 4 + 1)
                    elif n - 4 == HT - 1:
                        act.wait_ge(f_ready, DT)
                    else:
                        act.wait_ge(f_step, n - 4)
                    nc.scalar.copy(g_entry(half, k, 0), g_src(half, k)).then_inc(g_hi, 1)
                elif kind == "osplit":
                    _, half, o = step
                    act.wait_ge(oT_ready, UNITS if half else UNITS // 2)
                    if o == 0:
                        if half == 0:
                            wait_filled(act, ("exp", UNITS - 1, 5))
                        else:
                            wait_filled(act, ("wo", 0, DT - 1))
                    nc.scalar.copy(o_hi_tile(o), oT[:, o, half * HALF:(half + 1) * HALF]).then_inc(o_hi, 1)
                elif kind == "fin":
                    _, half, d = step
                    n = half * DT + d
                    act.wait_ge(f_ready, n + 1)
                    if n >= 2:
                        act.wait_ge(f_read, n - 1)
                    nc.scalar.activation(u_t[:, d % 2, :], bank[d][:], ACT.Tanh, scale=0.5).then_inc(ftanh, 1)

        @block.vector
        def _(dve):
            links = [0]

            def link(ins):
                links[0] += 1
                ins.then_inc(chain, 1)
                dve.wait_ge(chain, links[0])

            def layernorm(h):
                dve.wait_ge(x_in[h], 32)
                two = range(2 * h, 2 * h + 2)
                cols = slice(2 * h, 2 * h + 2)
                for i in two:
                    last = nc.vector.bn_stats(stats[:, i, :], x_tile(i))
                link(last)
                for i in two:
                    last = nc.vector.bn_aggr(mv[:, i, :], stats[:, i, :])
                link(last)
                nc.vector.tensor_scalar(lnv[:, 0, cols], mv[:, cols, 1], LN_EPS, None,
                                        ALU.add).then_inc(var_ready, 1)
                dve.wait_ge(std_ready, h + 1)
                link(nc.vector.reciprocal(lnv[:, 2, cols], lnv[:, 1, cols]))
                link(nc.vector.scalar_tensor_tensor(out=lnv[:, 3, cols], in0=lnv[:, 2, cols], scalar=-0.5,
                                                    in1=lnv[:, 2, cols], op0=ALU.mult, op1=ALU.mult))
                link(nc.vector.tensor_tensor(lnv[:, 4, cols], lnv[:, 3, cols], lnv[:, 0, cols], ALU.mult))
                link(nc.vector.scalar_tensor_tensor(out=lnv[:, 5, cols], in0=lnv[:, 4, cols], scalar=1.5,
                                                    in1=lnv[:, 2, cols], op0=ALU.add, op1=ALU.mult))
                for i in two:
                    nc.vector.tensor_scalar(xn_tile(i), x_tile(i), mv[:, i, 0:1], lnv[:, 5, i:i + 1],
                                            ALU.subtract, ALU.mult).then_inc(xn_ready, 1)

            nc.vector.memset(warm[:], 1.0).then_inc(warm_ready, 1)
            link(nc.vector.memset(vext[:], 0.0))
            link(nc.vector.memset(vext[:, :, HDIM:HDIM + 1], 1.0))
            link(nc.vector.memset(kst[96:P, :, :].bitcast(F32), 1.0))
            for step in steps:
                kind = step[0]
                if kind == "ln":
                    layernorm(step[1])
                elif kind == "xt":
                    i = step[1]
                    wait_filled(dve, step)
                    dve.wait_ge(xhi_ready, i + 1)
                    nc.vector.tensor_tensor(xsplit[:, 1, :, i * P:(i + 1) * P],
                                            aux(step)[:].rearrange("p (c t) -> p c t", c=DT),
                                            xsplit[:, 0, :, i * P:(i + 1) * P].bitcast(F32),
                                            ALU.subtract).then_inc(xlo_ready, 1)
                elif kind == "kv":
                    half = step[1]
                    cols = slice(half * HALF, (half + 1) * HALF)
                    wait_filled(dve, step)
                    dve.wait_ge(kv_copied, half + 1)
                    if half == 0:
                        dve.wait_ge(const_in, 48)
                    nc.vector.tensor_scalar(kst[96:P, half, :], kst[96:P, half, :].bitcast(F32),
                                            sel[96:P, half:half + 1], None, ALU.mult)
                    for e in range(2):
                        last = nc.vector.tensor_scalar(kst[0:96, e, cols], aux(step)[0:96, :],
                                                       sel[0:96, e:e + 1], None, ALU.mult)
                    link(last)
                    for e in range(2):
                        last = nc.vector.scalar_tensor_tensor(
                            out=kst[64:96, e, cols], in0=aux(step)[64:96, :], scalar=sel[64:96, e:e + 1],
                            in1=kst[64:96, e, cols].bitcast(F32), op0=ALU.mult, op1=ALU.subtract)
                    last.then_inc(k_ready, 1)
                elif kind == "vt":
                    half = step[1]
                    wait_filled(dve, step)
                    nc.vector.tensor_copy(
                        vext[:, 4 * half:4 * half + 4, 0:HDIM],
                        aux(step)[:, 0:4 * KV_ROWS].rearrange("p (i r) -> p i r", i=4)[:, :, 96:KV_ROWS]
                    ).then_inc(v_ready, 1)
                elif kind == "ba":
                    _, name, i = step
                    n = raw_no[step]
                    wait_filled(dve, step)
                    dve.wait_ge(raw_in[n % RAW_RING], 16 * (n // RAW_RING + 1))
                    m = merged_no[step]
                    if m >= 2:
                        before = list(merged_no)[m - 2]
                        dve.wait_ge(w_lo, split_no[before] + 1)
                    rows = hid_rows(i) if name == "w2" else P
                    ps = aux(step)[0:rows] if name == "w2" else aux(step)[:]
                    nc.vector.scalar_tensor_tensor(
                        out=cut(weff[:, m % 2, :], name, i), in0=cut(ps, name, i), scalar=LORA_SCALE,
                        in1=cut(raw[:, n % RAW_RING, :], name, i), op0=ALU.mult, op1=ALU.add
                    ).then_inc(merged, 1)
                elif kind == "q":
                    k = step[1]
                    wait_filled(dve, step)
                    dve.wait_ge(q_hi, k + 1)
                    nc.vector.tensor_tensor(qsplit[:, k % 2, 1, :], aux(step)[:],
                                            qsplit[:, k % 2, 0, :].bitcast(F32),
                                            ALU.subtract).then_inc(q_lo, 1)
                elif kind == "ffn1":
                    _, t, i = step
                    if i % 8 == 7:
                        half = i // 8
                        m = hid_rows(t)
                        dve.wait_ge(tanh_done, 2 * t + half + 1)
                        link(nc.vector.scalar_tensor_tensor(
                            out=u_t[0:m, half, :], in0=u_t[0:m, half, :], scalar=1.0, in1=bank[2 * half][0:m, :],
                            op0=ALU.add, op1=ALU.mult))
                        dve.wait_ge(h_ready, 4 * t + 2 * half + 2)
                        nc.vector.scalar_tensor_tensor(
                            out=g_src(half, t), in0=u_t[0:m, half, :], scalar=0.5, in1=bank[2 * half + 1][0:m, :],
                            op0=ALU.mult, op1=ALU.mult).then_inc(gate_done, 1)
                elif kind == "max":
                    _, u, k = step
                    wait_filled(dve, step)
                    if k < 4:
                        heads = [(aux(step)[:, e * SEQ:(e + 1) * SEQ], mask[:], rowmax[:, 1, k, e:e + 1])
                                 for e in range(2)]
                    else:
                        heads = [(aux(step)[:, n * P:(n + 1) * P], mask[:, P:2 * P],
                                  rowmax[:, 0, 2 * (k - 4) + n // 2, n % 2:n % 2 + 1]) for n in range(4)]
                    for scores, m, out in heads:
                        last = nc.vector.tensor_tensor_reduce(
                            out=scores, in0=scores, in1=m, scale=1.0, scalar=-3.0e38,
                            op0=ALU.add, op1=ALU.max, accum_out=out)
                    last.then_inc(max_done, 1)
                    if k == 5:
                        dve.wait_ge(max_done, 6 * u + 6)
                        if u >= 1:
                            wait_filled(dve, ("mrow", u - 1))
                        rm = rowmax[:].rearrange("p a j e -> p (a j) e")
                        ms = msplit[:].rearrange("p a j e -> p (a j) e")
                        link(nc.vector.tensor_scalar(ms[:, :, 0:2], rm, -1.0, None, ALU.mult))
                        nc.vector.scalar_tensor_tensor(
                            out=ms[:, :, 2:4], in0=rm, scalar=-1.0, in1=ms[:, :, 0:2].bitcast(F32),
                            op0=ALU.mult, op1=ALU.subtract).then_inc(m_ready, 1)
                elif kind == "olt":
                    u = step[1]
                    wait_filled(dve, step)
                    if u >= 1:
                        wait_filled(dve, ("ot", u - 1))
                    v = aux(step)[:].rearrange("p (e a j c) -> p e a j c", e=2, a=2, j=4)
                    link(nc.vector.reciprocal(rden[:], v[:, :, :, :, HDIM]))
                    for qt in range(2):
                        last = nc.vector.tensor_tensor(
                            on[:, qt, :].rearrange("p (j e c) -> p e j c", j=4, e=2),
                            v[:, :, qt, :, 0:HDIM],
                            rden[:, :, qt, :].unsqueeze(3).to_broadcast([P, 2, 4, HDIM]), ALU.mult)
                    last.then_inc(on_ready, 1)
                elif kind == "gsplit":
                    _, half, k = step
                    dve.wait_ge(g_hi, half * HT + k + 1)
                    nc.vector.tensor_tensor(g_entry(half, k, 1), g_src(half, k),
                                            g_entry(half, k, 0).bitcast(F32), ALU.subtract).then_inc(g_lo, 1)
                elif kind == "fin":
                    _, half, d = step
                    n = half * DT + d
                    r = raw_no[step]
                    gate = g[:, d, half * HALF:(half + 1) * HALF]
                    dve.wait_ge(ftanh, n + 1)
                    ins = nc.vector.scalar_tensor_tensor(out=gate, in0=u_t[:, d % 2, :], scalar=1.0,
                                                         in1=bank[d][:], op0=ALU.add, op1=ALU.mult)
                    ins.then_inc(f_read, 1)
                    dve.wait_ge(f_read, n + 1)
                    wait_filled(dve, ("wo", half, d))
                    if half == 1:
                        dve.wait_ge(y_out[d], 16)
                    ins = nc.vector.scalar_tensor_tensor(out=y[:, d, :], in0=gate, scalar=0.5,
                                                         in1=aux(("wo", half, d))[:], op0=ALU.mult, op1=ALU.mult)
                    ins.then_inc(s_read, 1)
                    dve.wait_ge(s_read, n + 1)
                    dve.wait_ge(raw_in[r % RAW_RING], 16 * (r // RAW_RING + 1))
                    nc.vector.tensor_tensor(y[:, d, :], y[:, d, :], raw[:, r % RAW_RING, :],
                                            ALU.add).then_inc(y_ready, 1)

        @block.gpsimd
        def _(pool):
            def lora_rows(step):
                _, r, part = step
                cols = lora_cols(r, part)
                done = lora_steps.index(step)
                his = sum(2 - s[2] for s in lora_steps[:done + 1])
                (first, first_raw), (second, second_raw) = lora_first[r], lora_second[r]
                pool.wait_ge(lora_hi, his)
                nc.gpsimd.tensor_tensor(second[0:32, cols], second_raw[0:32, cols],
                                        second[0:32, cols].bitcast(F32), ALU.subtract).then_inc(lora_lo, 1)
                pool.wait_ge(lora_lo, his - 1 + part)
                if part == 0:
                    nc.gpsimd.tensor_tensor(first[32:LROWS], first_raw[32:LROWS],
                                            first[32:LROWS].bitcast(F32), ALU.subtract).then_inc(lora_lo, 1)
                    pool.wait_ge(lora_lo, his)
                nc.gpsimd.tensor_copy(second[0:RANK, cols], second_raw[0:RANK, cols]).then_inc(lora_ready, 1)
                pool.wait_ge(lora_ready, done + 1)

            for step in steps:
                kind = step[0]
                if kind == "lora":
                    lora_rows(step)
                elif kind in ("w", "ba"):
                    pool.wait_ge(w_hi, split_no[step] + 1)
                    nc.gpsimd.tensor_tensor(split_dst(step, 1), split_src(step),
                                            split_dst(step, 0).bitcast(F32), ALU.subtract).then_inc(w_lo, 1)
                elif kind == "exp" and step[2] % 2 == 1:
                    _, u, k = step
                    pool.wait_ge(exp_done, 6 * u + k + 1)
                    if k == 1:
                        v = p1[:].rearrange("p e j q -> p (e j) q")
                    else:
                        v = p0[:, (k - 2) // 2].rearrange("p e j q -> p (e j) q")[:, :, 0:P]
                    nh = 8 if k == 1 else 4
                    nc.gpsimd.affine_select(out=v, in_=v, compare_op=ALU.is_ge, fill=0.0, base=0,
                                            pattern=[[0, nh], [1, P]], channel_multiplier=-1
                                            ).then_inc(p_masked, 1)
                elif kind == "osplit":
                    _, half, o = step
                    pool.wait_ge(o_hi, 4 * half + o + 1)
                    nc.gpsimd.tensor_tensor(o_lo_tile(o), oT[:, o, half * HALF:(half + 1) * HALF],
                                            o_hi_tile(o).bitcast(F32), ALU.subtract).then_inc(o_lo, 1)


def kernel(L0_attn_x, L0_attn_wq, L0_attn_wk, L0_attn_wv, L0_attn_wo, L0_ffn_w1, L0_ffn_w3, L0_ffn_w2,
           L0_ffn_lora_A1, L0_ffn_lora_B1, L0_ffn_lora_A3, L0_ffn_lora_B3, L0_ffn_lora_A2, L0_ffn_lora_B2):
    import concourse.bacc as bacc
    from concourse.bass_utils import run_bass_kernel_spmd

    x = np.ascontiguousarray(L0_attn_x).reshape(TOK, DIM)
    main = (HT - 1) * P

    def tiles(w):
        wt = np.asarray(w).T
        n = wt.shape[1] // P
        whole = wt[:, :n * P].reshape(DT, P, n, P).transpose(2, 1, 0, 3).reshape(n, P, DT * P)
        last = wt[:, n * P:].reshape(DT, P, -1).transpose(1, 0, 2)
        return whole, last

    w1, w1_last = tiles(L0_ffn_w1)
    w3, w3_last = tiles(L0_ffn_w3)
    wq, _ = tiles(np.asarray(L0_attn_wq).T)
    wkv = np.concatenate([np.asarray(L0_attn_wk)] * 6 + [np.asarray(L0_attn_wv)], axis=1)
    wkv = wkv.reshape(DT, P, KV_ROWS).transpose(1, 0, 2).reshape(P, DT * KV_ROWS)
    consts = np.zeros((P, 3 * P + 2), np.float32)
    consts[:, 0:P] = np.eye(P)
    consts[:, 2 * P:3 * P] = np.where(np.arange(P)[None, :] > np.arange(P)[:, None], NEG, 0.0)
    for e in range(2):
        consts[0:96, 3 * P + e] = (np.arange(96) // HDIM) % 2 == e
        consts[96:100, 3 * P + e] = np.arange(4) % 2 == e
    arrays = {
        "x": x, "xT": x.T, "wq": wq, "wkv": wkv, "wo": L0_attn_wo, "w1": w1, "w1_last": w1_last,
        "w3": w3, "w3_last": w3_last, "w2T": np.asarray(L0_ffn_w2).T,
        "A1": L0_ffn_lora_A1, "A3": L0_ffn_lora_A3, "B2T": np.asarray(L0_ffn_lora_B2).T,
        "B1T": np.asarray(L0_ffn_lora_B1).T, "B3T": np.asarray(L0_ffn_lora_B3).T, "A2": L0_ffn_lora_A2,
        "consts": consts,
    }
    for k in ("A1", "A3", "A2", "B1T", "B3T", "B2T"):
        arrays[k] = np.concatenate([np.asarray(arrays[k])] * 3, axis=0)
    arrays = {f"in_{k}": np.ascontiguousarray(v) for k, v in arrays.items()}
    nc = bacc.Bacc("TRN2", target_bir_lowering=False, num_devices=1)
    ap = {k[3:]: nc.dram_tensor(k, v.shape, F32, kind="ExternalInput").ap() for k, v in arrays.items()}
    outT = nc.dram_tensor("outT", (DIM, TOK), F32, kind="ExternalOutput").ap()
    mixed_block_kernel(nc, ap["x"], ap["xT"], ap["wq"], ap["wkv"], ap["wo"], ap["w1"], ap["w1_last"],
                       ap["w3"], ap["w3_last"], ap["w2T"], [ap["A1"], ap["A3"], ap["A2"]],
                       [ap["B1T"], ap["B3T"], ap["B2T"]], ap["consts"], outT)
    r = run_bass_kernel_spmd(nc, [arrays], core_ids=[0])
    return np.ascontiguousarray(r.results[0]["outT"].T).reshape(BATCH, SEQ, DIM)
```

```python
from contextlib import ExitStack

import numpy as np

import concourse.bass as bass
from concourse import mybir

F32 = mybir.dt.float32
F32R = mybir.dt.float32r
ALU = mybir.AluOpType
ACT = mybir.ActivationFunctionType

P = 128
BATCH, SEQ, DIM = 4, 256, 512
TOK = BATCH * SEQ
HALF = TOK // 2
HID, RANK = 1376, 16
HEADS, HDIM = 32, 16
DT = DIM // P
HT = -(-HID // P)
HLAST = HID - (HT - 1) * P
LORA_SCALE = 2.0
LN_EPS = 1e-5
SCORE_SCALE = float(HDIM) ** -0.5
NEG = -1.0e30
UNITS = BATCH * HEADS // 8
RAW_RING = 4
AUX0, AUX_RING = 4, 4
KV_ROWS = 6 * HDIM + HDIM
Q_DMAS = 12
M_DMAS = 4
LROWS = 3 * RANK
UPPER = 64
LORA_TILES = [(0, 1), (1, 5), (5, HT)]
KROWS = 100
WARM_UP = 4
PER_SLOT = 10


def hid_rows(t):
    return P if t < HT - 1 else HLAST


def unit(u):
    return u // 8, (u % 8) // 2, u % 2


def pieces(half, d):
    return 2 if (half, d) == (1, DT - 1) else 1


def piece_cols(step):
    _, half, d, piece = step
    n = HALF // pieces(half, d)
    return slice(piece * n, (piece + 1) * n)


def plan():
    def hidden(n):
        t, i = n // 16, n % 16
        group = [("ffn1", t, i)]
        if t + 1 < HT:
            group += {3: [("ba", "w13", 2 * t + 2)], 7: [("ba", "w13", 2 * t + 3)]}.get(i, [])
            if t + 2 == HT:
                group += {9: [("w", "lora2", 3)], 13: [("w", "lora2", 0)]}.get(i, [])
        else:
            group += {1: [("ba", "w2", 0)], 2: [("w", "lora2", 1)], 4: [("ba", "w2", 1)], 6: [("ba", "w2", 2)],
                      8: [("w", "lora2", 2)], 10: [("ba", "w2", 3)], 12: [("gsplit", 0, 0)],
                      14: [("gsplit", 0, 1)]}.get(i, [])
        return group

    def down(half):
        for k in range(HT):
            ahead = []
            if half == 0 and k + 4 < HT:
                ahead.append(("ba", "w2", k + 4))
            n = half * HT + k + 2
            if n < 2 * HT:
                ahead.append(("gsplit", n // HT, n % HT))
            if half == 0 and k >= HT - 4:
                ahead += [("w", "wo", k - HT + 4), ("osplit", 0, k - HT + 4)]
            if half == 1 and 1 <= k < 5:
                ahead.append(("osplit", 1, k - 1))
            if half == 0 and k < 2:
                order = [(0, 0), (0, 1)] if k == 0 else [(1, 0), (1, 1), (0, 2), (0, 3), (1, 2), (1, 3)]
            else:
                order = [(k, d) for d in range(DT)]
            yield ahead
            for kk, d in order:
                yield [("ffn2", half, kk, d)]

    def output(half):
        out = [("gate", half, d) for d in range(DT)]
        for d in range(DT):
            for piece in range(pieces(half, d)):
                out += [("wo", half, d, piece), ("fin", half, d, piece)]
        return out

    steps = [("bn", i) for i in range(4)]
    steps += [("stats", 0), ("ln", 0), ("w", "wkv", 0), ("lora", 0), ("xt", 0), ("xt", 1), ("xt", 2), ("xt", 3)]
    steps += [("xlo", i) for i in range(4)]
    steps += [("w", "wq", 0), ("lora", 1), ("kv", 0), ("bn", 4), ("bn", 5), ("ba", "w13", 0),
              ("ba", "w13", 1), ("kcopy", 0), ("bn", 6), ("bn", 7), ("stats", 1), ("ln", 1), ("q", 0)]
    for n in range(8):
        steps += hidden(n)
        steps += {2: [("xt", 4), ("xt", 5), ("klo", 0), ("xlo", 4), ("xlo", 5)],
                  4: [("xt", 6), ("xt", 7), ("xlo", 6), ("xlo", 7)], 6: [("lora", 2)]}.get(n, [])
    steps += [("kv", 1), ("kcopy", 1)]
    main = [hidden(n) for n in range(8, 16 * HT)] + [x for x in down(0) if x]
    at = 0
    for s in range(UNITS + 2):
        a, b, c = s, s - 1, s - 2
        for k in range(PER_SLOT):
            steps += main[at]
            at += 1
            if a < UNITS:
                steps += {0: [("max", a, 0)], 1: [("max", a, 1)], 2: [("max", a, 2)],
                          3: [("max", a, 3)], 4: [("max", a, 4)], 5: [("max", a, 5)],
                          8: [("mrow", a)]}.get(k, [])
            if 0 <= c < UNITS:
                steps += {2: [("pv", c)], 6: [("olt", c)], 9: [("ot", c)]}.get(k, [])
            if 0 <= b < UNITS:
                steps += {2: [("exp", b, 0)], 3: [("exp", b, 1)], 4: [("exp", b, 2)],
                          5: [("exp", b, 3)], 6: [("exp", b, 4)], 7: [("exp", b, 5)]}.get(k, [])
            if s == 0:
                steps += {6: [("vt", 0)], 8: [("krows", 0)]}.get(k, [])
            if s == 1:
                steps += {8: [("klo", 1)], 9: [("vt", 1)]}.get(k, [])
            if s % 2 == 0 and s // 2 + 1 < UNITS // 2:
                if k == 2 and s // 2 + 1 < 4:
                    steps.append(("w", "wq", s // 2 + 1))
                if k == 8:
                    steps.append(("q", s // 2 + 1))
    for group in main[at:]:
        steps += group
    steps += output(0)
    for group in down(1):
        steps += group
    steps += output(1)
    return steps


AUX_JOBS = {"xt", "kv", "vt", "ba", "q", "max", "mrow", "exp", "pv", "olt", "ot", "wo"}


def number(steps, kinds):
    return {s: n for n, s in enumerate(s for s in steps if s[0] in kinds)}


def mixed_block_kernel(nc, x, xT, wq, wkv, wo, w13T, w2T, A13, B13, lora2, consts, outT):
    steps = plan()
    aux_no = number(steps, AUX_JOBS)
    aux_steps = list(aux_no)
    split_no = number(steps, {"w", "ba"})
    merged_no = number(steps, {"ba"})
    fin_no = number(steps, {"fin"})
    raw_steps = [s for s in steps if s[0] in ("w", "ba", "gate")]
    raw_no = {s: n for n, s in enumerate(raw_steps)}

    with ExitStack() as ctx:
        def sb(name, shape, dt=F32):
            return ctx.enter_context(nc.sbuf_tensor(name, shape, dt))

        def sem(name):
            return ctx.enter_context(nc.semaphore(name))

        bank = [ctx.enter_context(nc.psum_tensor(f"bank{i}", [P, 512], F32)) for i in range(8)]

        ident = sb("ident", [P, P])
        mask_sel = sb("mask_sel", [P, 2 * P + 2])
        mask = mask_sel[:, 0:2 * P]
        sel = mask_sel[:, 2 * P:2 * P + 2]
        lora_b = sb("lora_b", [P, HT, 2, P], F32R)
        lora_a = sb("lora_a", [P, DIM], F32R)
        raw = sb("raw", [P, RAW_RING, 512])
        weff = sb("weff", [P, 2, 512])
        xsplit = sb("xsplit", [P, 2, DT, TOK], F32R)
        wq_s = sb("wq_s", [P, 4, 2, 512], F32R)
        w13 = sb("w13", [P, 2, 2, 2, 512], F32R)
        g = sb("g", [P, HT, TOK])
        u_t = sb("u_t", [P, 2, 512])
        qsplit = sb("qsplit", [P, 2, 2, 512], F32R)
        stack = [sb(f"stack{i}", [P, 4, 512], F32R) for i in range(2)]
        wkv_s = stack[1][:, 0:2, 0:DT * KV_ROWS].rearrange("p s (c m) -> p s c m", c=DT)
        kst = sb("kst", [P, 2, TOK], F32R)
        vext = sb("vext", [P, 8, 32])
        rowmax = sb("rowmax", [P, 2, 4, 2])
        mrow = sb("mrow", [16, SEQ])
        msplit = sb("msplit", [P, 2, 4, 4], F32R)
        p0 = sb("p0", [P, 2, 2, 2, SEQ])
        p1 = sb("p1", [P, 2, 4, P])
        ol = sb("ol", [P, 512])
        rden = sb("rden", [P, 2, 2, 4])
        on = sb("on", [P, 2, P])
        oT = sb("oT", [P, 4, TOK])
        stats = sb("stats", [P, 8, 6])
        mv = sb("mv", [P, 8, 2])
        lnv = sb("lnv", [P, 5, 8])
        warm = sb("warm", [P, 1])
        y = p0[:].rearrange("p a e b q -> p (a e b q)").rearrange("p (n t) -> p n t", n=4)

        const_in = sem("const_in")
        mask_in = sem("mask_in")
        k_rows_ready = sem("k_rows_ready")
        a13_in = sem("a13_in")
        b13_in = [sem(f"b13_in{i}") for i in range(len(LORA_TILES))]
        x_in = [sem(f"x_in{i}") for i in range(8)]
        raw_in = [sem(f"raw_in{i}") for i in range(RAW_RING)]
        q_moved = [sem(f"q_moved{i}") for i in range(2)]
        y_out = [sem(f"y_out{i}") for i in range(4)]
        aux_filled = sem("aux_filled")
        warm_ready = sem("warm_ready")
        lora_hi = sem("lora_hi")
        lora_lo = sem("lora_lo")
        m_moved = sem("m_moved")
        var_ready = sem("var_ready")
        std_ready = sem("std_ready")
        xn_ready = sem("xn_ready")
        xhi_ready = sem("xhi_ready")
        xlo_ready = sem("xlo_ready")
        kv_copied = sem("kv_copied")
        k_hi = sem("k_hi")
        k_ready = sem("k_ready")
        v_ready = sem("v_ready")
        merged = sem("merged")
        max_done = sem("max_done")
        s_read = sem("s_read")
        w_hi = sem("w_hi")
        w_lo = sem("w_lo")
        h_ready = sem("h_ready")
        tanh_done = sem("tanh_done")
        gate_done = sem("gate_done")
        q_hi = sem("q_hi")
        q_lo = sem("q_lo")
        m_ready = sem("m_ready")
        mrow_ready = sem("mrow_ready")
        exp_done = sem("exp_done")
        p_masked = sem("p_masked")
        ol_ready = sem("ol_ready")
        on_ready = sem("on_ready")
        oT_ready = sem("oT_ready")
        g_hi = sem("g_hi")
        g_lo = sem("g_lo")
        o_hi = sem("o_hi")
        o_lo = sem("o_lo")
        f_step = sem("f_step")
        f_ready = sem("f_ready")
        ftanh = sem("ftanh")
        f_read = sem("f_read")
        y_ready = sem("y_ready")
        chain = sem("chain")

        def x_tile(i):
            return g[:, 7 + i // 2, (i % 2) * 512:(i % 2) * 512 + 512]

        def xn_tile(i):
            return g[:, 3 + i // 2, (i % 2) * 512:(i % 2) * 512 + 512]

        kv_rows = g[0:KV_ROWS, 2, :]
        oT_flat = oT[:].rearrange("p o t -> p (o t)")
        b_raw = oT_flat[:, 0:HT * 2 * P].rearrange("p (t w m) -> p t w m", t=HT, w=2)
        a_raw = oT_flat[:, HT * 2 * P:HT * 2 * P + DIM]
        lora_b_flat = lora_b[:].rearrange("p t w m -> p (t w m)")
        a2 = lora_b_flat[0:LROWS, 0:HID]
        b2T = lora_b_flat[0:LROWS, 3 * 512:3 * 512 + DIM]

        def wait_read(eng, step):
            kind, *at = step
            last_reader = {
                "xt": lambda i: (xlo_ready, i + 1),
                "kv": lambda half: (k_hi, half + 1),
                "vt": lambda half: (v_ready, half + 1),
                "ba": lambda name, i: (merged, merged_no[step] + 1),
                "q": lambda k: (q_lo, k + 1),
                "max": lambda u, k: (max_done, 6 * u + k + 1),
                "mrow": lambda u: (mrow_ready, u + 1),
                "exp": lambda u, k: (exp_done, 6 * u + k + 1),
                "pv": lambda u: (ol_ready, u + 1),
                "olt": lambda u: (on_ready, u + 1),
                "ot": lambda u: (oT_ready, u + 1),
                "wo": lambda half, d, piece: (s_read, DT * half + d + piece + 1),
            }
            eng.wait_ge(*last_reader[kind](*at))

        def wait_filled(eng, step):
            eng.wait_ge(aux_filled, aux_no[step] + 1)

        def aux(step):
            return bank[AUX0 + aux_no[step] % AUX_RING]

        def split_dst(step, part):
            _, name, i = step
            if name == "wkv":
                return wkv_s[:, part]
            if name == "wq":
                return wq_s[:, i, part, :]
            if name == "wo":
                return stack[part][:, i, :]
            if name == "lora2":
                return lora_b_flat[lora2_rows(i, part), i * 512:i * 512 + lora2_cols(i)]
            if name == "w2":
                if i < 4:
                    return wq_s[0:hid_rows(i), i, part, :]
                j = i - 4
                return xsplit[0:hid_rows(i), part, j // 2, (j % 2) * 512:(j % 2) * 512 + 512]
            t, h = i // 2, i % 2
            return w13[:, t % 2, :, part, 2 * h * P:2 * (h + 1) * P].rearrange("p w (c m) -> p c w m", c=2)

        def lora2_rows(i, part):
            if part == 0:
                return slice(0, LROWS)
            return slice(2 * RANK, LROWS) if i < 3 else slice(0, RANK)

        def lora2_cols(i):
            return min(512, HID - i * 512) if i < 3 else DIM

        def split_src(step, part):
            kind, name, i = step
            if kind == "ba":
                tile = weff[:, merged_no[step] % 2, :]
            else:
                tile = raw[:, raw_no[step] % RAW_RING, :]
            if name == "wkv":
                return tile[:, 0:DT * KV_ROWS].rearrange("p (c m) -> p c m", c=DT)
            if name == "w13":
                return tile.rearrange("p (c w m) -> p c w m", c=2, w=2)
            if name == "w2":
                return tile[0:hid_rows(i)]
            if name == "lora2":
                return tile[lora2_rows(i, part), 0:lora2_cols(i)]
            return tile

        def g_entry(half, k, part):
            n = (half * HT + k) % 4
            return w13[0:hid_rows(k), (n // 2 + 1) % 2, n % 2, part, :]

        def g_src(half, k):
            return g[0:hid_rows(k), k, half * HALF:(half + 1) * HALF]

        def gate_tile(half, d):
            return g[:, d, half * HALF:(half + 1) * HALF]

        def o_hi_tile(o):
            return kst[:, o // 2, (o % 2) * 512:(o % 2) * 512 + 512]

        def o_lo_tile(o):
            return qsplit[:, o // 2, o % 2, :]

        block = ctx.enter_context(nc.Block())

        @block.sync
        def _(sp):
            def load_x(i):
                sp.dma_start(x_tile(i), x[i * P:(i + 1) * P, :]).then_inc(x_in[i], 16)

            def load_raw(step):
                n = raw_no[step]
                if n >= RAW_RING:
                    old = raw_steps[n - RAW_RING]
                    if old[0] == "w":
                        sp.wait_ge(w_lo, split_no[old] + 1)
                    elif old[0] == "ba":
                        sp.wait_ge(merged, merged_no[old] + 1)
                    else:
                        sp.wait_ge(y_ready, fin_no[("fin", old[1], old[2], 0)] + 1)
                kind, name, i = step
                tile = raw[:, n % RAW_RING, :]
                if kind == "gate":
                    half, d = name, i
                    src = xT[d * P:(d + 1) * P, half * HALF:(half + 1) * HALF]
                    dst = tile
                elif name == "wkv":
                    src, dst = wkv, tile[:, 0:DT * KV_ROWS]
                elif name == "wq":
                    src, dst = wq[i], tile
                elif name == "wo":
                    src, dst = wo[i * P:(i + 1) * P, :], tile
                elif name == "w2":
                    src, dst = w2T[i * P:i * P + hid_rows(i), :], tile[0:hid_rows(i)]
                elif name == "lora2":
                    cols = lora2_cols(i)
                    src, dst = lora2[:, i * 512:i * 512 + cols], tile[0:LROWS, 0:cols]
                else:
                    src, dst = w13T[i], tile
                sp.dma_start(dst, src).then_inc(raw_in[n % RAW_RING], 16)

            def move_queries(k):
                sp.wait_ge(q_hi, k + 1)
                if k >= 2:
                    wait_filled(sp, ("exp", 2 * (k - 2) + 1, 5))
                for blk, part in ((0, 0), (2, 0), (1, 1)):
                    if part == 1:
                        sp.wait_ge(q_lo, k + 1)
                    for j in range(4):
                        sp.dma_start(stack[k % 2][32 * blk:32 * blk + 32, j, :].bitcast(F32),
                                     qsplit[32 * j:32 * j + 32, k % 2, part, :].bitcast(F32)
                                     ).then_inc(q_moved[k % 2], 16)

            def move_maxima(u):
                b2 = u % 2
                sp.wait_ge(mrow_ready, u + 1)
                for j in range(4):
                    sp.dma_start(stack[(u // 2) % 2][96:100, j, b2 * SEQ:(b2 + 1) * SEQ].bitcast(F32),
                                 mrow[4 * j:4 * j + 4, :]).then_inc(m_moved, 16)

            def load_B13(part):
                t0, t1 = LORA_TILES[part]
                sp.dma_start(b_raw[:, t0:t1], B13[:, t0:t1]).then_inc(b13_in[part], 16)

            for i in range(4):
                load_x(i)
            sp.dma_start(ident[:], consts[:, 0:P]).then_inc(const_in, 16)
            load_raw(raw_steps[0])
            load_B13(0)
            sp.dma_start(a_raw, A13).then_inc(a13_in, 16)
            load_raw(raw_steps[1])
            sp.dma_start(mask_sel[:], consts[:, P:3 * P + 2]).then_inc(mask_in, 16)
            load_raw(raw_steps[2])
            load_raw(raw_steps[3])
            load_B13(1)
            for i in range(4, 8):
                load_x(i)
            load_B13(2)
            for step in steps:
                if step in raw_no and raw_no[step] + RAW_RING < len(raw_steps):
                    load_raw(raw_steps[raw_no[step] + RAW_RING])
                if step[0] == "q":
                    move_queries(step[1])
                if step[0] == "mrow":
                    move_maxima(step[1])
                if step[0] == "fin":
                    _, half, d, _ = step
                    cols = piece_cols(step)
                    t0 = half * HALF
                    sp.wait_ge(y_ready, fin_no[step] + 1)
                    sp.dma_start(outT[d * P:(d + 1) * P, t0 + cols.start:t0 + cols.stop],
                                 y[:, d, cols]).then_inc(y_out[d], 16)
            for d in range(DT):
                sp.wait_ge(y_out[d], 16 * (pieces(0, d) + pieces(1, d)))

        @block.tensor
        def _(pe):
            def take_bank(step):
                n = aux_no[step]
                if n >= AUX_RING:
                    wait_read(pe, aux_steps[n - AUX_RING])
                return aux(step)

            def three_passes(out, w_parts, m_parts, start, stop):
                pe.matmul(out, w_parts[0], m_parts[0], start=start, stop=False)
                pe.matmul(out, w_parts[0], m_parts[1], start=False, stop=False)
                return pe.matmul(out, w_parts[1], m_parts[0], start=False, stop=stop)

            def x_parts(c, half):
                return [xsplit[:, part, c, half * HALF:(half + 1) * HALF] for part in (0, 1)]

            def xt(step):
                i = step[1]
                ps = take_bank(step)
                pe.wait_ge(xn_ready, i + 1)
                for c in range(DT):
                    mm = pe.transpose(ps[:, c * P:(c + 1) * P], xn_tile(i)[:, c * P:(c + 1) * P], ident[:])
                mm.then_inc(aux_filled, 1)

            def kv(step):
                half = step[1]
                ps = take_bank(step)
                pe.wait_ge(xhi_ready, 4 * (half + 1))
                pe.wait_ge(w_lo, split_no[("w", "wkv", 0)] + 1)
                for w_part, m_part in ((0, 0), (1, 0), (0, 1)):
                    if m_part == 1:
                        pe.wait_ge(xlo_ready, 4 * (half + 1))
                    for c in range(DT):
                        mm = pe.matmul(ps[0:KV_ROWS, :], wkv_s[:, w_part, c, :], x_parts(c, half)[m_part],
                                       start=(w_part, m_part, c) == (0, 0, 0), stop=(m_part, c) == (1, DT - 1))
                mm.then_inc(aux_filled, 1)

            def vt(step):
                half = step[1]
                ps = take_bank(step)
                pe.wait_ge(kv_copied, half + 1)
                for i in range(4):
                    t0 = half * HALF + i * P
                    mm = pe.transpose(ps[:, i * KV_ROWS:(i + 1) * KV_ROWS], kv_rows[:, t0:t0 + P],
                                      ident[0:KV_ROWS, 0:KV_ROWS])
                mm.then_inc(aux_filled, 1)

            def ba(step):
                _, name, i = step
                ps = take_bank(step)
                if name == "w2":
                    pe.wait_ge(w_lo, split_no[("w", "lora2", 3)] + 1)
                    pe.wait_ge(w_lo, split_no[("w", "lora2", i // 4)] + 1)
                    m = hid_rows(i)
                    mm = pe.matmul(ps[0:m, :], a2[:, i * P:i * P + m], b2T, start=True, stop=True)
                else:
                    t, h = i // 2, i % 2
                    part = [t in range(*p) for p in LORA_TILES].index(True)
                    pe.wait_ge(lora_lo, 2 * part + 4)
                    rows = UPPER + LROWS
                    for c in range(2):
                        mm = pe.matmul(ps[:, c * 2 * P:(c + 1) * 2 * P],
                                       lora_a[0:rows, (2 * h + c) * P:(2 * h + c + 1) * P],
                                       lora_b[0:rows, t, :, :], start=True, stop=True)
                mm.then_inc(aux_filled, 1)

            def q(step):
                half, o, _ = unit(2 * step[1])
                ps = take_bank(step)
                pe.wait_ge(w_lo, split_no[("w", "wq", o)] + 1)
                for c in range(DT):
                    mm = three_passes(ps[:, :], [wq_s[:, o, part, c * P:(c + 1) * P] for part in (0, 1)],
                                      x_parts(c, half), c == 0, c == DT - 1)
                mm.then_inc(aux_filled, 1)

            def ffn1(step):
                _, t, i = step
                half, w, c = i // 8, (i // 4) % 2, i % 4
                m = hid_rows(t)
                if i == 0:
                    pe.wait_ge(w_lo, split_no[("ba", "w13", 2 * t)] + 1)
                if i == 2:
                    pe.wait_ge(w_lo, split_no[("ba", "w13", 2 * t + 1)] + 1)
                if t == 0 and i % 8 == 0:
                    pe.wait_ge(xlo_ready, 4 * (half + 1))
                if c == 0 and t >= 1:
                    pe.wait_ge(gate_done, 2 * (t - 1) + half + 1)
                ps = bank[2 * half + w]
                mm = three_passes(ps[0:m, :], [w13[:, t % 2, w, part, c * P:c * P + m] for part in (0, 1)],
                                  x_parts(c, half), c == 0, c == DT - 1)
                if c == DT - 1:
                    mm.then_inc(h_ready, 1)

            def causal_scores(step):
                _, u, k = step
                half, o, b2 = unit(u)
                kcol = (2 * half + b2) * SEQ
                st = stack[(u // 2) % 2]
                ps = take_bank(step)
                if k == 0:
                    pe.wait_ge(q_moved[(u // 2) % 2], 16 * Q_DMAS * (u // 4 + 1))
                    pe.wait_ge(k_ready, half + 1)
                if k < 4:
                    mm = pe.matmul(ps[:, :], st[0:96, k, b2 * SEQ + P:b2 * SEQ + 2 * P],
                                   kst[0:96, :, kcol:kcol + SEQ], start=True, stop=True)
                else:
                    for n in range(2):
                        mm = pe.matmul(ps[:, 256 * n:256 * n + 256],
                                       st[0:96, 2 * (k - 4) + n, b2 * SEQ:b2 * SEQ + P],
                                       kst[0:96, :, kcol:kcol + P], start=True, stop=True)
                mm.then_inc(aux_filled, 1)

            def max_rows(step):
                u = step[1]
                ps = take_bank(step)
                pe.wait_ge(m_ready, u + 1)
                for qt in range(2):
                    mm = pe.transpose(ps[0:16, qt * P:(qt + 1) * P],
                                      msplit[:, qt].rearrange("p j r -> p (j r)").bitcast(F32), ident[:])
                mm.then_inc(aux_filled, 1)

            def shifted_scores(step):
                _, u, k = step
                half, o, b2 = unit(u)
                kcol = (2 * half + b2) * SEQ
                st = stack[(u // 2) % 2]
                ps = take_bank(step)
                if u == 0 and k == 0:
                    pe.wait_ge(k_rows_ready, 2)
                if k == 0:
                    pe.wait_ge(m_moved, 16 * M_DMAS * (u + 1))
                if k < 2:
                    mm = pe.matmul(ps[:, :], kst[0:KROWS, k, kcol + P:kcol + 2 * P],
                                   st[0:KROWS, :, b2 * SEQ + P:b2 * SEQ + 2 * P], start=True, stop=True)
                else:
                    pp, e = (k - 2) // 2, (k - 2) % 2
                    mm = pe.matmul(ps[:, :], kst[0:KROWS, e, kcol:kcol + P],
                                   st[0:KROWS, 2 * pp:2 * pp + 2, b2 * SEQ:(b2 + 1) * SEQ],
                                   start=True, stop=True)
                mm.then_inc(aux_filled, 1)

            def pv(step):
                u = step[1]
                half, o, b2 = unit(u)
                kt = 2 * (2 * half + b2)
                ps = take_bank(step)
                pe.wait_ge(v_ready, half + 1)
                pe.wait_ge(p_masked, 3 * (u + 1))
                for j in range(4):
                    pe.matmul(ps[32 * j:32 * j + 32, :], vext[:, kt, :], p0[:, j // 2, :, j % 2, :],
                              start=True, stop=False)
                for j in range(4):
                    out = ps[32 * j:32 * j + 32, :].rearrange("p (e q) -> p e q", e=2)[:, :, P:2 * P]
                    mm = pe.matmul(out, vext[:, kt + 1, :], p1[:, :, j, :], start=False, stop=True)
                mm.then_inc(aux_filled, 1)

            def olt(step):
                u = step[1]
                ps = take_bank(step)
                pe.wait_ge(ol_ready, u + 1)
                for n in range(4):
                    mm = pe.transpose(ps[:, n * P:(n + 1) * P], ol[:, n * P:(n + 1) * P], ident[:])
                mm.then_inc(aux_filled, 1)

            def ot(step):
                u = step[1]
                ps = take_bank(step)
                pe.wait_ge(on_ready, u + 1)
                for qt in range(2):
                    mm = pe.transpose(ps[:, qt * P:(qt + 1) * P], on[:, qt, :], ident[:])
                mm.then_inc(aux_filled, 1)

            def ffn2(step):
                _, half, k, d = step
                m = hid_rows(k)
                if half == 0 and k == 0 and d % 2 == 0:
                    pe.wait_ge(gate_done, 2 * HT - 1 + d // 2)
                if d == 0:
                    pe.wait_ge(g_lo, half * HT + k + 1)
                    if half == 0:
                        pe.wait_ge(w_lo, split_no[("ba", "w2", k)] + 1)
                if k == 0 and half == 1:
                    pe.wait_ge(f_read, d + 1)
                w = [split_dst(("ba", "w2", k), part)[:, d * P:(d + 1) * P] for part in (0, 1)]
                mm = three_passes(bank[d][:, :], w, [g_entry(half, k, part) for part in (0, 1)],
                                  k == 0, k == HT - 1)
                if k == HT - 1:
                    mm.then_inc(f_ready, 1)
                elif d == DT - 1:
                    mm.then_inc(f_step, 1)

            def out_proj(step):
                _, half, d, _ = step
                cols = piece_cols(step)
                ps = take_bank(step)
                if d == 0:
                    pe.wait_ge(o_lo, 4 * (half + 1))
                    pe.wait_ge(w_lo, split_no[("w", "wo", 3)] + 1)
                for o in range(4):
                    mm = three_passes(ps[:, cols], [stack[part][:, o, d * P:(d + 1) * P] for part in (0, 1)],
                                      [o_hi_tile(o)[:, cols], o_lo_tile(o)[:, cols]], o == 0, o == 3)
                mm.then_inc(aux_filled, 1)

            pe.wait_ge(warm_ready, 1)
            for _ in range(WARM_UP):
                pe.matmul(bank[0][:, :], u_t[:, 0, 0:P], u_t[:, 0, :], start=True, stop=True)
            pe.wait_ge(const_in, 16)
            do = {"xt": xt, "kv": kv, "vt": vt, "ba": ba, "q": q, "ffn1": ffn1, "max": causal_scores,
                  "mrow": max_rows, "exp": shifted_scores, "pv": pv, "olt": olt, "ot": ot,
                  "ffn2": ffn2, "wo": out_proj}
            for step in steps:
                if step[0] in do:
                    do[step[0]](step)

        @block.scalar
        def _(act):
            def split_weight(step):
                kind, name, i = step
                if kind == "ba":
                    act.wait_ge(merged, merged_no[step] + 1)
                else:
                    n = raw_no[step]
                    act.wait_ge(raw_in[n % RAW_RING], 16 * (n // RAW_RING + 1))
                if name == "w13" and i >= 4:
                    act.wait_ge(h_ready, 4 * (i // 2 - 1))
                if name == "lora2" and i == 0:
                    wait_filled(act, ("ba", "w13", 2 * HT - 1))
                if name == "w2" and i == 0:
                    wait_filled(act, ("q", UNITS // 2 - 1))
                if name == "w2" and i == 4:
                    act.wait_ge(h_ready, 4 * HT)
                if name == "wo" and i == 0:
                    wait_filled(act, ("exp", UNITS - 1, 5))
                nc.scalar.copy(split_dst(step, 0), split_src(step, 0)).then_inc(w_hi, 1)

            def split_lora(part):
                t0, t1 = LORA_TILES[part]
                if part == 0:
                    act.wait_ge(a13_in, 16)
                    nc.scalar.copy(lora_a[:], a_raw).then_inc(lora_hi, 1)
                act.wait_ge(b13_in[part], 16)
                nc.scalar.copy(lora_b[:, t0:t1], b_raw[:, t0:t1]).then_inc(lora_hi, 1)

            act.wait_ge(warm_ready, 1)
            nc.scalar.activation(warm[:], u_t[:, 0, 0:1], ACT.Sqrt)
            for step in steps:
                kind = step[0]
                if kind == "stats":
                    h = step[1]
                    act.wait_ge(var_ready, h + 1)
                    nc.scalar.activation(lnv[:, 4, 4 * h:4 * h + 4], lnv[:, 0, 4 * h:4 * h + 4],
                                         ACT.Sqrt).then_inc(std_ready, 1)
                elif kind == "lora":
                    split_lora(step[1])
                elif kind in ("w", "ba"):
                    split_weight(step)
                elif kind == "xt":
                    i = step[1]
                    wait_filled(act, step)
                    nc.scalar.copy(xsplit[:, 0, :, i * P:(i + 1) * P],
                                   aux(step)[:].rearrange("p (c t) -> p c t", c=DT)).then_inc(xhi_ready, 1)
                elif kind == "kcopy":
                    half = step[1]
                    step = ("kv", half)
                    wait_filled(act, step)
                    nc.scalar.copy(kv_rows[:, half * HALF:(half + 1) * HALF],
                                   aux(step)[0:KV_ROWS, :]).then_inc(kv_copied, 1)
                    if half == 0:
                        act.wait_ge(mask_in, 16)
                    for e in range(2):
                        last = nc.scalar.activation(kst[0:96, e, half * HALF:(half + 1) * HALF],
                                                    aux(step)[0:96, :], ACT.Copy, scale=sel[0:96, e:e + 1])
                    last.then_inc(k_hi, 1)
                elif kind == "q":
                    k = step[1]
                    wait_filled(act, step)
                    if k >= 2:
                        act.wait_ge(q_moved[k % 2], 16 * Q_DMAS * (k // 2))
                    nc.scalar.copy(qsplit[:, k % 2, 0, :], aux(step)[:]).then_inc(q_hi, 1)
                elif kind == "ffn1":
                    _, t, i = step
                    if i % 8 == 3:
                        half = i // 8
                        m = hid_rows(t)
                        act.wait_ge(h_ready, 4 * t + 2 * half + 1)
                        nc.scalar.activation(u_t[0:m, half, :], bank[2 * half][0:m, :], ACT.Tanh,
                                             scale=0.5).then_inc(tanh_done, 1)
                elif kind == "mrow":
                    u = step[1]
                    wait_filled(act, step)
                    if u >= 1:
                        act.wait_ge(m_moved, 16 * M_DMAS * u)
                    nc.scalar.copy(mrow[:], aux(step)[0:16, 0:SEQ]).then_inc(mrow_ready, 1)
                elif kind == "exp":
                    _, u, k = step
                    wait_filled(act, step)
                    if k == 0 and u >= 1:
                        wait_filled(act, ("pv", u - 1))
                    if k < 2:
                        out = p1[:, k].rearrange("p j q -> p (j q)")
                    else:
                        out = p0[:, (k - 2) // 2, (k - 2) % 2].rearrange("p j q -> p (j q)")
                    nc.scalar.activation(out, aux(step)[:], ACT.Exp, scale=SCORE_SCALE
                                         ).then_inc(exp_done, 1)
                elif kind == "pv":
                    u = step[1]
                    wait_filled(act, step)
                    if u >= 1:
                        wait_filled(act, ("olt", u - 1))
                    nc.scalar.copy(ol[:], aux(step)[:]).then_inc(ol_ready, 1)
                elif kind == "ot":
                    half, o, b2 = unit(step[1])
                    t0 = (2 * half + b2) * SEQ
                    wait_filled(act, step)
                    nc.scalar.copy(oT[:, o, t0:t0 + SEQ], aux(step)[:, 0:SEQ]
                                   ).then_inc(oT_ready, 1)
                elif kind == "gsplit":
                    _, half, k = step
                    n = half * HT + k
                    act.wait_ge(gate_done, 2 * k + half + 1)
                    if n < 4:
                        act.wait_ge(h_ready, 4 * (HT - 1) if n < 2 else 4 * HT)
                    elif n - 4 < HT - 1:
                        act.wait_ge(f_step, n - 4 + 1)
                    elif n - 4 == HT - 1:
                        act.wait_ge(f_ready, DT)
                    else:
                        act.wait_ge(f_step, n - 4)
                    nc.scalar.copy(g_entry(half, k, 0), g_src(half, k)).then_inc(g_hi, 1)
                elif kind == "osplit":
                    _, half, o = step
                    act.wait_ge(oT_ready, UNITS if half else UNITS // 2)
                    if o == 0:
                        if half == 0:
                            wait_filled(act, ("exp", UNITS - 1, 5))
                        else:
                            wait_filled(act, ("wo", 0, DT - 1, 0))
                    nc.scalar.copy(o_hi_tile(o), oT[:, o, half * HALF:(half + 1) * HALF]).then_inc(o_hi, 1)
                elif kind == "gate":
                    _, half, d = step
                    n = half * DT + d
                    act.wait_ge(f_ready, n + 1)
                    if n >= 2:
                        act.wait_ge(f_read, n - 1)
                    nc.scalar.activation(u_t[:, n % 2, :], bank[d][:], ACT.Tanh, scale=0.5).then_inc(ftanh, 1)

        @block.vector
        def _(dve):
            links = [0]
            bn_last = [None]

            def link(ins):
                links[0] += 1
                ins.then_inc(chain, 1)
                dve.wait_ge(chain, links[0])

            def statistics(h):
                link(bn_last[0])
                for i in range(4 * h, 4 * h + 4):
                    last = nc.vector.bn_aggr(mv[:, i, :], stats[:, i, :])
                link(last)
                cols = slice(4 * h, 4 * h + 4)
                nc.vector.tensor_scalar(lnv[:, 0, cols], mv[:, cols, 1], LN_EPS, None,
                                        ALU.add).then_inc(var_ready, 1)

            def layernorm(h):
                cols = slice(4 * h, 4 * h + 4)
                var, root, t = lnv[:, 0, cols], lnv[:, 1, cols], lnv[:, 2, cols]
                dve.wait_ge(std_ready, h + 1)
                link(nc.vector.reciprocal(root, lnv[:, 4, cols]))
                link(nc.vector.scalar_tensor_tensor(out=t, in0=root, scalar=-0.5, in1=root,
                                                    op0=ALU.mult, op1=ALU.mult))
                link(nc.vector.tensor_tensor(t, t, var, ALU.mult))
                link(nc.vector.scalar_tensor_tensor(out=lnv[:, 3, cols], in0=t, scalar=1.5, in1=root,
                                                    op0=ALU.add, op1=ALU.mult))
                for i in range(4 * h, 4 * h + 4):
                    nc.vector.tensor_scalar(xn_tile(i), x_tile(i), mv[:, i, 0:1], lnv[:, 3, i:i + 1],
                                            ALU.subtract, ALU.mult).then_inc(xn_ready, 1)

            nc.vector.memset(u_t[:, 0, :], 0.0).then_inc(warm_ready, 1)
            link(nc.vector.memset(kst[96:P, :, :].bitcast(F32), 1.0))
            link(nc.vector.memset(vext[:], 0.0))
            link(nc.vector.memset(vext[:, :, HDIM:HDIM + 1], 1.0))
            for step in steps:
                kind = step[0]
                if kind == "bn":
                    i = step[1]
                    dve.wait_ge(x_in[i], 16)
                    bn_last[0] = nc.vector.bn_stats(stats[:, i, :], x_tile(i))
                elif kind == "stats":
                    statistics(step[1])
                elif kind == "ln":
                    layernorm(step[1])
                elif kind == "xlo":
                    i = step[1]
                    step = ("xt", i)
                    wait_filled(dve, step)
                    dve.wait_ge(xhi_ready, i + 1)
                    nc.vector.tensor_tensor(xsplit[:, 1, :, i * P:(i + 1) * P],
                                            aux(step)[:].rearrange("p (c t) -> p c t", c=DT),
                                            xsplit[:, 0, :, i * P:(i + 1) * P].bitcast(F32),
                                            ALU.subtract).then_inc(xlo_ready, 1)
                elif kind == "klo":
                    half = step[1]
                    if half == 0:
                        dve.wait_ge(mask_in, 16)
                    cols = slice(half * HALF, (half + 1) * HALF)
                    dve.wait_ge(k_hi, half + 1)
                    for e in range(2):
                        last = nc.vector.scalar_tensor_tensor(
                            out=kst[64:96, e, cols], in0=kv_rows[64:96, cols], scalar=sel[64:96, e:e + 1],
                            in1=kst[64:96, e, cols].bitcast(F32), op0=ALU.mult, op1=ALU.subtract)
                    last.then_inc(k_ready, 1)
                elif kind == "krows":
                    for e in range(2):
                        nc.vector.tensor_scalar(kst[96:P, e, :], kst[96:P, e, :].bitcast(F32),
                                                sel[96:P, e:e + 1], None, ALU.mult).then_inc(k_rows_ready, 1)
                elif kind == "vt":
                    half = step[1]
                    wait_filled(dve, step)
                    nc.vector.tensor_copy(
                        vext[:, 4 * half:4 * half + 4, 0:HDIM],
                        aux(step)[:, 0:4 * KV_ROWS].rearrange("p (i r) -> p i r", i=4)[:, :, 96:KV_ROWS]
                    ).then_inc(v_ready, 1)
                elif kind == "ba":
                    _, name, i = step
                    n = raw_no[step]
                    wait_filled(dve, step)
                    dve.wait_ge(raw_in[n % RAW_RING], 16 * (n // RAW_RING + 1))
                    m = merged_no[step]
                    if m >= 2:
                        before = list(merged_no)[m - 2]
                        dve.wait_ge(w_lo, split_no[before] + 1)
                    whole = slice(0, hid_rows(i) if name == "w2" else P)
                    nc.vector.scalar_tensor_tensor(
                        out=weff[whole, m % 2, :], in0=aux(step)[whole, :], scalar=LORA_SCALE,
                        in1=raw[whole, n % RAW_RING, :], op0=ALU.mult, op1=ALU.add).then_inc(merged, 1)
                elif kind == "q":
                    k = step[1]
                    wait_filled(dve, step)
                    dve.wait_ge(q_hi, k + 1)
                    nc.vector.tensor_tensor(qsplit[:, k % 2, 1, :], aux(step)[:],
                                            qsplit[:, k % 2, 0, :].bitcast(F32),
                                            ALU.subtract).then_inc(q_lo, 1)
                elif kind == "ffn1":
                    _, t, i = step
                    if i % 8 == 7:
                        half = i // 8
                        m = hid_rows(t)
                        dve.wait_ge(tanh_done, 2 * t + half + 1)
                        link(nc.vector.scalar_tensor_tensor(
                            out=u_t[0:m, half, :], in0=u_t[0:m, half, :], scalar=1.0, in1=bank[2 * half][0:m, :],
                            op0=ALU.add, op1=ALU.mult))
                        dve.wait_ge(h_ready, 4 * t + 2 * half + 2)
                        nc.vector.scalar_tensor_tensor(
                            out=g_src(half, t), in0=u_t[0:m, half, :], scalar=0.5, in1=bank[2 * half + 1][0:m, :],
                            op0=ALU.mult, op1=ALU.mult).then_inc(gate_done, 1)
                elif kind == "max":
                    _, u, k = step
                    wait_filled(dve, step)
                    if k < 4:
                        heads = [(aux(step)[:, e * SEQ:(e + 1) * SEQ], mask[:], rowmax[:, 1, k, e:e + 1])
                                 for e in range(2)]
                    else:
                        heads = [(aux(step)[:, n * P:(n + 1) * P], mask[:, P:2 * P],
                                  rowmax[:, 0, 2 * (k - 4) + n // 2, n % 2:n % 2 + 1]) for n in range(4)]
                    for scores, m, out in heads:
                        last = nc.vector.tensor_tensor_reduce(
                            out=scores, in0=scores, in1=m, scale=1.0, scalar=-3.0e38,
                            op0=ALU.add, op1=ALU.max, accum_out=out)
                    last.then_inc(max_done, 1)
                    if k == 5:
                        dve.wait_ge(max_done, 6 * u + 6)
                        if u >= 1:
                            wait_filled(dve, ("mrow", u - 1))
                        rm = rowmax[:].rearrange("p a j e -> p (a j) e")
                        ms = msplit[:].rearrange("p a j e -> p (a j) e")
                        link(nc.vector.tensor_scalar(ms[:, :, 0:2], rm, -1.0, None, ALU.mult))
                        nc.vector.scalar_tensor_tensor(
                            out=ms[:, :, 2:4], in0=rm, scalar=-1.0, in1=ms[:, :, 0:2].bitcast(F32),
                            op0=ALU.mult, op1=ALU.subtract).then_inc(m_ready, 1)
                elif kind == "olt":
                    u = step[1]
                    wait_filled(dve, step)
                    if u >= 1:
                        wait_filled(dve, ("ot", u - 1))
                    v = aux(step)[:].rearrange("p (e a j c) -> p e a j c", e=2, a=2, j=4)
                    link(nc.vector.reciprocal(rden[:], v[:, :, :, :, HDIM]))
                    for qt in range(2):
                        last = nc.vector.tensor_tensor(
                            on[:, qt, :].rearrange("p (j e c) -> p e j c", j=4, e=2),
                            v[:, :, qt, :, 0:HDIM],
                            rden[:, :, qt, :].unsqueeze(3).to_broadcast([P, 2, 4, HDIM]), ALU.mult)
                    last.then_inc(on_ready, 1)
                elif kind == "gsplit":
                    _, half, k = step
                    dve.wait_ge(g_hi, half * HT + k + 1)
                    nc.vector.tensor_tensor(g_entry(half, k, 1), g_src(half, k),
                                            g_entry(half, k, 0).bitcast(F32), ALU.subtract).then_inc(g_lo, 1)
                elif kind == "gate":
                    _, half, d = step
                    n = half * DT + d
                    dve.wait_ge(ftanh, n + 1)
                    nc.vector.scalar_tensor_tensor(out=gate_tile(half, d), in0=u_t[:, n % 2, :], scalar=1.0,
                                                   in1=bank[d][:], op0=ALU.add, op1=ALU.mult).then_inc(f_read, 1)
                elif kind == "fin":
                    _, half, d, piece = step
                    cols = piece_cols(step)
                    n = fin_no[step]
                    r = raw_no[("gate", half, d)]
                    wait_filled(dve, ("wo", half, d, piece))
                    dve.wait_ge(f_read, half * DT + d + 1)
                    if half == 1:
                        dve.wait_ge(y_out[d], 16)
                    nc.vector.scalar_tensor_tensor(
                        out=y[:, d, cols], in0=gate_tile(half, d)[:, cols], scalar=0.5,
                        in1=aux(("wo", half, d, piece))[:, cols], op0=ALU.mult, op1=ALU.mult).then_inc(s_read, 1)
                    dve.wait_ge(s_read, n + 1)
                    dve.wait_ge(raw_in[r % RAW_RING], 16 * (r // RAW_RING + 1))
                    nc.vector.tensor_tensor(y[:, d, cols], y[:, d, cols], raw[:, r % RAW_RING, cols],
                                            ALU.add).then_inc(y_ready, 1)

        @block.gpsimd
        def _(pool):
            def lora_rows(part):
                t0, t1 = LORA_TILES[part]
                jobs = []
                for w, base in enumerate((0, UPPER)):
                    jobs.append((lora_b[base:base + RANK, t0:t1, w, :], b_raw[base:base + RANK, t0:t1, w, :]))
                    if part == 0:
                        rows = slice(base + 2 * RANK, base + LROWS)
                        jobs.append((lora_a[rows], a_raw[rows]))
                pool.wait_ge(lora_hi, part + 2)
                done = 0 if part == 0 else 2 * part + 2
                for n, (split, whole) in enumerate(jobs):
                    last = nc.gpsimd.tensor_tensor(split, whole, split.bitcast(F32), ALU.subtract)
                    last.then_inc(lora_lo, 1)
                    pool.wait_ge(lora_lo, done + n + 1)

            for step in steps:
                kind = step[0]
                if kind == "lora":
                    lora_rows(step[1])
                elif kind in ("w", "ba"):
                    pool.wait_ge(w_hi, split_no[step] + 1)
                    if step[1] == "lora2":
                        pool.wait_ge(w_lo, split_no[step])
                        pool.wait_ge(p_masked, sum(s[0] == "exp" and s[2] % 2 == 1
                                                   for s in steps[:steps.index(step)]))
                    lo = split_dst(step, 1)
                    nc.gpsimd.tensor_tensor(lo, split_src(step, 1), lo.bitcast(F32) if step[1] == "lora2"
                                            else split_dst(step, 0).bitcast(F32), ALU.subtract
                                            ).then_inc(w_lo, 1)
                    if step[1] == "lora2":
                        pool.wait_ge(w_lo, split_no[step] + 1)
                elif kind == "exp" and step[2] % 2 == 1:
                    _, u, k = step
                    pool.wait_ge(exp_done, 6 * u + k + 1)
                    if k == 1:
                        v = p1[:].rearrange("p e j q -> p (e j) q")
                    else:
                        v = p0[:, (k - 2) // 2].rearrange("p e j q -> p (e j) q")[:, :, 0:P]
                    nh = 8 if k == 1 else 4
                    nc.gpsimd.affine_select(out=v, in_=v, compare_op=ALU.is_ge, fill=0.0, base=0,
                                            pattern=[[0, nh], [1, P]], channel_multiplier=-1
                                            ).then_inc(p_masked, 1)
                elif kind == "osplit":
                    _, half, o = step
                    pool.wait_ge(o_hi, 4 * half + o + 1)
                    nc.gpsimd.tensor_tensor(o_lo_tile(o), oT[:, o, half * HALF:(half + 1) * HALF],
                                            o_hi_tile(o).bitcast(F32), ALU.subtract).then_inc(o_lo, 1)


def kernel(L0_attn_x, L0_attn_wq, L0_attn_wk, L0_attn_wv, L0_attn_wo, L0_ffn_w1, L0_ffn_w3, L0_ffn_w2,
           L0_ffn_lora_A1, L0_ffn_lora_B1, L0_ffn_lora_A3, L0_ffn_lora_B3, L0_ffn_lora_A2, L0_ffn_lora_B2):
    import concourse.bacc as bacc
    from concourse.bass_utils import run_bass_kernel_spmd

    x = np.ascontiguousarray(L0_attn_x).reshape(TOK, DIM)

    def padded(a, rows, cols):
        a = np.asarray(a)
        return np.pad(a, ((0, rows - a.shape[0]), (0, cols - a.shape[1])))

    w13 = np.stack([padded(np.asarray(w).T, DIM, HT * P) for w in (L0_ffn_w1, L0_ffn_w3)])
    w13 = w13.reshape(2, 2, 2, P, HT, P).transpose(4, 1, 3, 2, 0, 5).reshape(2 * HT, P, 4 * P)
    wq = np.asarray(L0_attn_wq).reshape(DT, P, 4, P).transpose(2, 1, 0, 3).reshape(4, P, DT * P)
    wkv = np.concatenate([np.asarray(L0_attn_wk)] * 6 + [np.asarray(L0_attn_wv)], axis=1)
    wkv = wkv.reshape(DT, P, KV_ROWS).transpose(1, 0, 2).reshape(P, DT * KV_ROWS)
    consts = np.zeros((P, 3 * P + 2), np.float32)
    consts[:, 0:P] = np.eye(P)
    consts[:, 2 * P:3 * P] = np.where(np.arange(P)[None, :] > np.arange(P)[:, None], NEG, 0.0)
    for e in range(2):
        consts[0:96, 3 * P + e] = (np.arange(96) // HDIM) % 2 == e
        consts[96:100, 3 * P + e] = np.arange(4) % 2 == e
    A13 = np.zeros((P, DIM), np.float32)
    B13 = np.zeros((P, HT, 2, P), np.float32)
    for w, (a, b) in enumerate(((L0_ffn_lora_A1, L0_ffn_lora_B1), (L0_ffn_lora_A3, L0_ffn_lora_B3))):
        rows = slice(w * UPPER, w * UPPER + LROWS)
        A13[rows] = np.concatenate([np.asarray(a)] * 3)
        B13[rows, :, w] = np.concatenate([padded(np.asarray(b).T, RANK, HT * P)] * 3).reshape(LROWS, HT, P)
    lora2 = np.concatenate([padded(L0_ffn_lora_A2, RANK, 3 * 512), np.asarray(L0_ffn_lora_B2).T], axis=1)
    arrays = {
        "x": x, "xT": x.T, "wq": wq, "wkv": wkv, "wo": L0_attn_wo, "w13T": w13, "w2T": np.asarray(L0_ffn_w2).T,
        "A13": A13, "B13": B13, "lora2": np.concatenate([lora2] * 3),
        "consts": consts,
    }
    arrays = {f"in_{k}": np.ascontiguousarray(v) for k, v in arrays.items()}
    nc = bacc.Bacc("TRN2", target_bir_lowering=False, num_devices=1)
    ap = {k[3:]: nc.dram_tensor(k, v.shape, F32, kind="ExternalInput").ap() for k, v in arrays.items()}
    outT = nc.dram_tensor("outT", (DIM, TOK), F32, kind="ExternalOutput").ap()
    mixed_block_kernel(nc, ap["x"], ap["xT"], ap["wq"], ap["wkv"], ap["wo"], ap["w13T"], ap["w2T"], ap["A13"],
                       ap["B13"], ap["lora2"], ap["consts"], outT)
    r = run_bass_kernel_spmd(nc, [arrays], core_ids=[0])
    return np.ascontiguousarray(r.results[0]["outT"].T).reshape(BATCH, SEQ, DIM)
```
